# Optimizing a Trainium2 kernel written in Bass

```python
import numpy as np
import jax
import jax.numpy as jnp

def _softmax(x, axis=-1):
    return jax.nn.softmax(x, axis=axis)

def _gelu(x):
    return jax.nn.gelu(x, approximate=True)

def _silu(x):
    return jax.nn.silu(x)

def _sigmoid(x):
    return jax.nn.sigmoid(x)

def _layernorm(x, axis=-1, eps=1e-05):
    m = jnp.mean(x, axis=axis, keepdims=True)
    v = jnp.var(x, axis=axis, keepdims=True)
    return (x - m) / jnp.sqrt(v + eps)

def _scatter_add(tgt, idx, src, axis=0):
    return tgt.at[idx].add(src)

def _segment_sum(src, seg, n):
    return jax.ops.segment_sum(src, seg, n)
kernel_name = 'mk_gnn_ffn_d1_gnn_r8_4c6cfe'

def setup_inputs(seed: int=0):
    np.random.seed(seed)
    _w = jnp.asarray

    def _rec_inputs():
        import jax
        import jax.numpy as jnp
        _gk = jax.random.key(seed)
        x = -0.0005963 + 1.001 * jax.random.normal(jax.random.fold_in(_gk, 1), (384, 1024), jnp.float32)
        src = jax.random.randint(jax.random.fold_in(_gk, 2), (6144,), 0, 384, jnp.int32)
        dst = jax.random.randint(jax.random.fold_in(_gk, 3), (6144,), 0, 384, jnp.int32)
        _o = jnp.argsort(dst, stable=True)
        src = src[_o]
        dst = dst[_o]
        edge_type_5 = jax.random.randint(jax.random.fold_in(_gk, 12), (6144,), 0, 5, jnp.int32)
        return (x, src, dst, edge_type_5)
    x, src, dst, edge_type_5 = _rec_inputs()

    def _L0_gnn_setup():
        import jax, jax.numpy as jnp
        import numpy as np
        N = 384
        E = 12288
        IN_F = 1024
        OUT_F = 1024
        H = 16
        D = OUT_F // H
        NUM_ETYPES = 4

        def _build_mask(edge_index, edge_type, edge_type_weights, dtype):
            src, dst = (edge_index[0], edge_index[1])
            w = jax.nn.softplus(edge_type_weights)
            mask = jnp.full((N, N), -jnp.inf, dtype=dtype)
            mask = mask.at[src, dst].set(w[edge_type - 1])
            diag = jnp.diagonal(mask)
            idx = jnp.arange(N)
            mask = mask.at[idx, idx].set(jnp.where(jnp.isneginf(diag), w[3], diag))
            return mask
        key = jax.random.key(seed)
        ks = jax.random.split(key, 20)
        p = lambda k, shape: jax.random.normal(k, shape, dtype=jnp.float32) * 0.02
        return {'x': jax.random.normal(ks[0], (N, IN_F), dtype=jnp.float32), 'edge_index': jax.random.randint(ks[1], (2, E), 0, N), 'edge_type': jax.random.randint(ks[2], (E,), 1, NUM_ETYPES + 1), 'edge_type_weights': jnp.ones((NUM_ETYPES,), jnp.float32) + 0.1 * jax.random.normal(ks[3], (NUM_ETYPES,), dtype=jnp.float32), 'wq': p(ks[4], (OUT_F, IN_F)), 'bq': p(ks[5], (OUT_F,)), 'wk': p(ks[6], (OUT_F, IN_F)), 'bk': p(ks[7], (OUT_F,)), 'wv': p(ks[8], (OUT_F, IN_F)), 'bv': p(ks[9], (OUT_F,)), 'wiq': p(ks[10], (OUT_F, OUT_F)), 'biq': p(ks[11], (OUT_F,)), 'wik': p(ks[12], (OUT_F, OUT_F)), 'bik': p(ks[13], (OUT_F,)), 'wiv': p(ks[14], (OUT_F, OUT_F)), 'biv': p(ks[15], (OUT_F,)), 'wo': p(ks[16], (OUT_F, OUT_F)), 'bo': p(ks[17], (OUT_F,))}
    _L0_gnn_all = _L0_gnn_setup()
    _L0_gnn_in = {k: v for k, v in _L0_gnn_all.items() if k in ('edge_type_weights', 'wq', 'bq', 'wk', 'bk', 'wv', 'bv', 'wiq', 'biq', 'wik', 'bik', 'wiv', 'biv', 'wo', 'bo')}
    del _L0_gnn_all

    def _L0_ffn_setup():
        import jax, jax.numpy as jnp
        import numpy as np
        QMAX = 127.0

        def _ste_round(v):
            return v + jax.lax.stop_gradient(jnp.round(v) - v)

        def _act_fake_quant(x, clip_factor):
            scale = jax.nn.sigmoid(clip_factor) * jnp.max(jnp.abs(x)) / QMAX
            return jnp.clip(_ste_round(x / scale), -QMAX - 1.0, QMAX) * scale

        def _weight_fake_quant(w):
            scale = jnp.max(jnp.abs(w), axis=1, keepdims=True) / QMAX
            return jnp.clip(_ste_round(w / scale), -QMAX - 1.0, QMAX) * scale
        key = jax.random.key(seed)
        k1, k2, k3, k4 = jax.random.split(key, 4)
        B, S, H, I = (8, 1024, 1024, 352)
        return {'x': jax.random.normal(k1, (B, S, H), dtype=jnp.float32), 'clip_x': jnp.full((1,), 4.0, dtype=jnp.float32), 'clip_down': jnp.full((1,), 4.0, dtype=jnp.float32), 'w_gate': jax.random.normal(k2, (I, H), dtype=jnp.float32) * 0.02, 'w_up': jax.random.normal(k3, (I, H), dtype=jnp.float32) * 0.02, 'w_down': jax.random.normal(k4, (H, I), dtype=jnp.float32) * 0.02}
    _L0_ffn_all = _L0_ffn_setup()
    _L0_ffn_in = {k: v for k, v in _L0_ffn_all.items() if k in ('clip_x', 'clip_down', 'w_gate', 'w_up', 'w_down')}
    del _L0_ffn_all
    return {'x': x, 'src': src, 'dst': dst, 'edge_type_5': edge_type_5, 'L0_gnn_edge_type_weights': _L0_gnn_in['edge_type_weights'], 'L0_gnn_wq': _L0_gnn_in['wq'], 'L0_gnn_bq': _L0_gnn_in['bq'], 'L0_gnn_wk': _L0_gnn_in['wk'], 'L0_gnn_bk': _L0_gnn_in['bk'], 'L0_gnn_wv': _L0_gnn_in['wv'], 'L0_gnn_bv': _L0_gnn_in['bv'], 'L0_gnn_wiq': _L0_gnn_in['wiq'], 'L0_gnn_biq': _L0_gnn_in['biq'], 'L0_gnn_wik': _L0_gnn_in['wik'], 'L0_gnn_bik': _L0_gnn_in['bik'], 'L0_gnn_wiv': _L0_gnn_in['wiv'], 'L0_gnn_biv': _L0_gnn_in['biv'], 'L0_gnn_wo': _L0_gnn_in['wo'], 'L0_gnn_bo': _L0_gnn_in['bo'], 'L0_ffn_clip_x': _L0_ffn_in['clip_x'], 'L0_ffn_clip_down': _L0_ffn_in['clip_down'], 'L0_ffn_w_gate': _L0_ffn_in['w_gate'], 'L0_ffn_w_up': _L0_ffn_in['w_up'], 'L0_ffn_w_down': _L0_ffn_in['w_down']}

def reference(x, src, dst, edge_type_5, L0_gnn_edge_type_weights, L0_gnn_wq, L0_gnn_bq, L0_gnn_wk, L0_gnn_bk, L0_gnn_wv, L0_gnn_bv, L0_gnn_wiq, L0_gnn_biq, L0_gnn_wik, L0_gnn_bik, L0_gnn_wiv, L0_gnn_biv, L0_gnn_wo, L0_gnn_bo, L0_ffn_clip_x, L0_ffn_clip_down, L0_ffn_w_gate, L0_ffn_w_up, L0_ffn_w_down):
    import jax
    import jax.numpy as jnp

    def _L0_gnn_ref(x, edge_index, edge_type, edge_type_weights, wq, bq, wk, bk, wv, bv, wiq, biq, wik, bik, wiv, biv, wo, bo):
        import jax, jax.numpy as jnp
        import numpy as np
        N = 384
        E = 12288
        IN_F = 1024
        OUT_F = 1024
        H = 16
        D = OUT_F // H
        NUM_ETYPES = 4

        def _build_mask(edge_index, edge_type, edge_type_weights, dtype):
            src, dst = (edge_index[0], edge_index[1])
            w = jax.nn.softplus(edge_type_weights)
            mask = jnp.full((N, N), -jnp.inf, dtype=dtype)
            mask = mask.at[src, dst].set(w[edge_type - 1])
            diag = jnp.diagonal(mask)
            idx = jnp.arange(N)
            mask = mask.at[idx, idx].set(jnp.where(jnp.isneginf(diag), w[3], diag))
            return mask
        q = x @ wq.T + bq
        k = x @ wk.T + bk
        v = x @ wv.T + bv
        q2 = (q @ wiq.T + biq).reshape(N, H, D).transpose(1, 0, 2)
        k2 = (k @ wik.T + bik).reshape(N, H, D).transpose(1, 0, 2)
        v2 = (v @ wiv.T + biv).reshape(N, H, D).transpose(1, 0, 2)
        mask = _build_mask(edge_index, edge_type, edge_type_weights, x.dtype)
        scale = 1.0 / np.sqrt(D).astype(np.float32)
        scores = jnp.einsum('hnd,hmd->hnm', q2, k2) * scale + mask[None]
        attn = jax.nn.softmax(scores, axis=-1)
        out = jnp.einsum('hnm,hmd->hnd', attn, v2)
        out = out.transpose(1, 0, 2).reshape(N, OUT_F)
        return out @ wo.T + bo

    def _L0_ffn_ref(x, clip_x, clip_down, w_gate, w_up, w_down):
        import jax, jax.numpy as jnp
        import numpy as np
        QMAX = 127.0

        def _ste_round(v):
            return v + jax.lax.stop_gradient(jnp.round(v) - v)

        def _act_fake_quant(x, clip_factor):
            scale = jax.nn.sigmoid(clip_factor) * jnp.max(jnp.abs(x)) / QMAX
            return jnp.clip(_ste_round(x / scale), -QMAX - 1.0, QMAX) * scale

        def _weight_fake_quant(w):
            scale = jnp.max(jnp.abs(w), axis=1, keepdims=True) / QMAX
            return jnp.clip(_ste_round(w / scale), -QMAX - 1.0, QMAX) * scale
        xq = _act_fake_quant(x, clip_x[0])
        gate = jnp.einsum('bsh,ih->bsi', xq, _weight_fake_quant(w_gate))
        up = jnp.einsum('bsh,ih->bsi', xq, _weight_fake_quant(w_up))
        h = _act_fake_quant(jax.nn.silu(gate) * up, clip_down[0])
        return jnp.einsum('bsi,hi->bsh', h, _weight_fake_quant(w_down))
    edge_index = jnp.stack([src, dst])
    x = x + _L0_gnn_ref(_layernorm(x, axis=-1), edge_index, edge_type_5, L0_gnn_edge_type_weights, L0_gnn_wq, L0_gnn_bq, L0_gnn_wk, L0_gnn_bk, L0_gnn_wv, L0_gnn_bv, L0_gnn_wiq, L0_gnn_biq, L0_gnn_wik, L0_gnn_bik, L0_gnn_wiv, L0_gnn_biv, L0_gnn_wo, L0_gnn_bo)
    x = x + _L0_ffn_ref(_layernorm(x, axis=-1)[None], L0_ffn_clip_x, L0_ffn_clip_down, L0_ffn_w_gate, L0_ffn_w_up, L0_ffn_w_down)[0]
    return x

_drawn_inputs = setup_inputs


def setup_inputs(seed=0):
    import zlib

    import numpy as np

    out = dict(_drawn_inputs(seed))
    spreads = {}
    factors = {'L0_gnn_edge_type_weights': 5.514,
     'L0_gnn_wq': 4.033,
     'L0_gnn_bq': 8.0,
     'L0_gnn_wk': 4.033,
     'L0_gnn_bk': 8.0,
     'L0_gnn_bv': 4.962,
     'L0_gnn_wiq': 4.017,
     'L0_gnn_biq': 8.0,
     'L0_gnn_wik': 4.004,
     'L0_gnn_bik': 8.0,
     'L0_gnn_biv': 3.618}
    for name, (base, spread) in spreads.items():
        noise = np.random.default_rng([zlib.crc32(name.encode()), seed]).standard_normal(out[name].shape)
        drawn = base * np.exp(spread * noise) if base else spread * noise
        out[name] = jnp.asarray(drawn.astype(out[name].dtype))
    for name, factor in factors.items():
        out[name] = (out[name] * factor).astype(out[name].dtype)
    return out
```

```python
from contextlib import ExitStack

import concourse.bass as bass
from concourse import mybir

P = 128
ALU = mybir.AluOpType
ACT = mybir.ActivationFunctionType
AX = mybir.AxisListType
F32 = mybir.dt.float32
F32R = mybir.dt.float32r
BF16 = mybir.dt.bfloat16
F16 = mybir.dt.float16
I32 = mybir.dt.int32

RING = 4
AHEAD = 2
HOT_RING = 4
ROUND = 1.5 * 2.0 ** 23
QMAX = 127.0
NO_EDGE = -1.0e30
EPS = 1e-5
HEADS = 16
FEATURE_MAJOR = 5
FFN_JOBS = [("gate_up", 0), ("gate_up", 1), ("gate_up", 2), ("down", 0), ("down", 1)]


def gnn_ffn(nc, x, weights, bias_cols, bo, edge_cols, edge_rows, type_weights, clips, w_gate_up, w_down, out):
    N, F = x.shape
    NT = N // P
    KT = F // P
    HALF = F // 2
    D = F // HEADS
    EC = edge_cols.shape[2]
    SPAN = P // 2
    IT = w_gate_up.shape[0] // 2
    I = w_down.shape[2]
    SCALE = float(D) ** -0.5
    UNITS = weights.shape[0]
    GROUPS = KT // RING
    assert NT == 3 and KT == 8 and D == 64 and UNITS == 7 * KT and IT * P <= N

    with ExitStack() as ctx:
        def sb(name, shape, dt, stack=ctx):
            return stack.enter_context(nc.sbuf_tensor(name, shape, dt))

        def sem(name):
            return ctx.enter_context(nc.semaphore(name))

        bank = [ctx.enter_context(nc.psum_tensor(f"bank{b}", [P, 512], F32)) for b in range(8)]

        rows = sb("rows", [P, NT, F], F32)
        raw = [sb(f"raw{r}", [P, F], F32) for r in range(RING)]
        w_hi = [sb(f"w_hi{r}", [P, F], F32R) for r in range(RING)]
        w_lo = [sb(f"w_lo{r}", [P, F], F32R) for r in range(RING)]
        mask = sb("mask", [P, NT, N], F32)
        gate_upT = sb("gate_upT", [P, KT, 2, IT * P], BF16)
        downT = sb("downT", [P, IT, F], BF16)
        ident = sb("ident", [P, P], F32)
        ident_b = sb("ident_b", [P, P], BF16)
        ones = sb("ones", [P, P], F32)
        bias = sb("bias", [P, 6, KT], F32)
        bo_all = sb("bo_all", [P, F], F32)
        stats = sb("stats", [P, NT, 2, 6], F32)
        mean_var = sb("mean_var", [P, NT, 2], F32)
        newton = sb("newton", [P, 4, NT], F32)
        bits = sb("bits", [P, 2, NT], I32)
        row_max = sb("row_max", [P, 2, NT], F32)
        neg_max = sb("neg_max", [P, 2, NT], F32)
        row_sum = sb("row_sum", [P, 2, NT], F32)
        row_inv = sb("row_inv", [P, 2, NT], F32)
        type_w = sb("type_w", [P, 5, 4], F32)
        clip = sb("clip", [P, 4, 2], F32)
        gate_up_scale = sb("gate_up_scale", [P, IT, 2], F32)
        down_scale = sb("down_scale", [P, KT], F32)
        q_inv = sb("q_inv", [P, 4], F32)
        extremes = sb("extremes", [P, 2, NT, 2], F32)
        top = sb("top", [P, 24], F32)
        act_scale = sb("act_scale", [P, 3, IT], F32)

        with ExitStack() as early:
            key_parts = sb("key_parts", [P, 2, 192], I32, early)
            keys = sb("keys", [P, 192], F32, early)
            same = sb("same", [P, P - 1], F32, early)
            overridden = sb("overridden", [P, SPAN], BF16, early)
            dup = sb("dup", [P, P], BF16, early)
            fold = sb("fold", [P, EC], BF16, early)
            edge_i = sb("edge_i", [P, 3, EC], I32, early)
            edge_f = sb("edge_f", [P, 3, EC], F32, early)
            code = sb("code", [P, 3, EC], F32, early)
            place = sb("place", [P, EC], I32, early)
            count = sb("count", [P, N], F16, early)
            loops = sb("loops", [P, NT, N], BF16, early)
            loop_code = sb("loop_code", [P, P], BF16, early)
            src_hot = [sb(f"src_hot{r}", [P, N], BF16, early) for r in range(HOT_RING)]
            dst_hot = [sb(f"dst_hot{r}", [P, N], BF16, early) for r in range(HOT_RING)]
            classes = sb("classes", [P, NT, N], I32, early)
            picked = sb("picked", [P, NT, N], F32, early)
        with ExitStack() as late:
            turned = sb("turned", [P, KT, N], F32, late)
            xqT = sb("xqT", [P, KT, N], BF16, late)
            gate_e = sb("gate_e", [P, IT, N], F32, late)
            gate_s = sb("gate_s", [P, IT, N], F32, late)
            hidden = sb("hidden", [P, IT, N], F32, late)
            hqT = sb("hqT", [P, IT, N], BF16, late)
            diagonals = sb("diagonals", [P, F], F32, late)
            spread = sb("spread", [P, F], F32, late)
        k2_hi = sb("k2_hi", [P, KT, N], F32R)
        k2_lo = sb("k2_lo", [P, KT, N], F32R)
        q2_hi = sb("q2_hi", [P, KT, N], F32R)
        q2_lo = sb("q2_lo", [P, KT, N], F32R)

        with ExitStack() as late:
            normed2 = sb("normed2", [P, NT, F], F32, late)
            ffn_out = sb("ffn_out", [P, NT, F], F32, late)
        xT_hi = sb("xT_hi", [P, KT, N], F32R)
        xT_lo = sb("xT_lo", [P, KT, N], F32R)
        v2_hi = xT_hi[:].rearrange("p a b -> p (a b)").rearrange("p (m f) -> p m f", m=NT)
        v2_lo = xT_lo[:].rearrange("p a b -> p (a b)").rearrange("p (m f) -> p m f", m=NT)

        with ExitStack() as early:
            normed = sb("normed", [P, NT, F], F32, early)
        yT_hi = sb("yT_hi", [P, KT, N], F32R)
        yT_lo = sb("yT_lo", [P, KT, N], F32R)

        with ExitStack() as early:
            ffn_raw = sb("ffn_raw", [P, 2 * F], F32, early)
            ffn_int = sb("ffn_int", [P, 2 * F], BF16, early)
        probs = [sb(f"probs{b}", [P, NT, N], F32) for b in range(2)]
        pT_hi = sb("pT_hi", [P, NT, N], F32R)
        pT_lo = sb("pT_lo", [P, NT, N], F32R)

        x_landed = [sem(f"x_landed{m}") for m in range(NT)]
        consts_landed = sem("consts_landed")
        edges_landed = sem("edges_landed")
        bo_landed = sem("bo_landed")
        w_landed = [sem(f"w_landed{r}") for r in range(RING)]
        ffn_landed = sem("ffn_landed")
        ident_ready = sem("ident_ready")
        edge_consts = sem("edge_consts")
        dve_step = sem("dve_step")
        act_step = sem("act_step")
        pool_step = sem("pool_step")
        compared = sem("compared")
        dup_ready = sem("dup_ready")
        dead_ready = sem("dead_ready")
        hot_ready = sem("hot_ready")
        hot_used = sem("hot_used")
        mask_summed = sem("mask_summed")
        classes_ready = sem("classes_ready")
        softplus_exp = sem("softplus_exp")
        type_w_ready = sem("type_w_ready")
        mask_ready = sem("mask_ready")
        norm_ready = sem("norm_ready")
        norm_turned = sem("norm_turned")
        xT_hi_ready = sem("xT_hi_ready")
        xT_ready = sem("xT_ready")
        hi_split = sem("hi_split")
        lo_split = sem("lo_split")
        unit_done = sem("unit_done")
        y_hi_ready = sem("y_hi_ready")
        y_ready = sem("y_ready")
        ffn_scaled = sem("ffn_scaled")
        ffn_rounded = sem("ffn_rounded")
        ffn_turned = sem("ffn_turned")
        ffn_ready = sem("ffn_ready")
        v2_done = sem("v2_done")
        v2_hi_ready = sem("v2_hi_ready")
        v2_ready = sem("v2_ready")
        scores_done = sem("scores_done")
        scored = sem("scored")
        neg_ready = sem("neg_ready")
        exp_ready = sem("exp_ready")
        inv_ready = sem("inv_ready")
        probs_ready = sem("probs_ready")
        probs_turned = sem("probs_turned")
        pT_hi_ready = sem("pT_hi_ready")
        pT_ready = sem("pT_ready")
        values_done = sem("values_done")
        o_hi_ready = sem("o_hi_ready")
        o_ready = sem("o_ready")
        residual_ready = sem("residual_ready")
        wo_done = sem("wo_done")
        norm2_ready = sem("norm2_ready")
        norm2_turned = sem("norm2_turned")
        top_ready = sem("top_ready")
        top_row = sem("top_row")
        top_one = sem("top_one")
        top_all = sem("top_all")
        quant_ready = sem("quant_ready")
        x_rounded = sem("x_rounded")
        xq_ready = sem("xq_ready")
        gate_up_done = sem("gate_up_done")
        gate_exp = sem("gate_exp")
        h_rounded = sem("h_rounded")
        hq_ready = sem("hq_ready")
        down_done = sem("down_done")
        diagonals_ready = sem("diagonals_ready")
        spread_done = sem("spread_done")
        spread_ready = sem("spread_ready")
        ffn_out_ready = sem("ffn_out_ready")
        out_ready = sem("out_ready")
        stored = sem("stored")

        MASK_BANK = (7, 5, 6)
        V2_BANKS = ((5, 6, 4), (0, 1, 2))

        def unit(p, g, r):
            return g * RING + (p * KT + r)

        block = ctx.enter_context(nc.Block())

        @block.sync
        def _(sp):
            for m in range(NT):
                sp.dma_start(rows[:, m, :], x.rearrange("(m p) f -> p m f", p=P)[:, m, :]).then_inc(x_landed[m], 16)
            for r in range(RING):
                sp.dma_start(raw[r][:], weights[r]).then_inc(w_landed[r], 16)
            with sp.Fori(1, UNITS // RING) as g:
                for r in range(RING):
                    sp.wait_ge(hi_split, g * RING + (r + 1 - RING))
                    sp.wait_ge(lo_split, g * RING + (r + 1 - RING))
                    sp.dma_start(raw[r][:], weights[bass.ds(g * RING + r, 1)].rearrange("a p f -> (a p) f")) \
                        .then_inc(w_landed[r], 16)
            for m in range(NT):
                for h in range(2):
                    s = slice(h * HALF, (h + 1) * HALF)
                    sp.wait_ge(out_ready, 2 * m + h + 1)
                    sp.dma_start(out.rearrange("(m p) f -> p m f", p=P)[:, m, s], rows[:, m, s]).then_inc(stored, 16)
            sp.wait_ge(stored, 16 * NT * 2)

        @block.gpsimd
        def _(pool):
            steps = [0]

            def step(ins):
                ins.then_inc(pool_step, 1)
                steps[0] += 1
                pool.wait_ge(pool_step, steps[0])

            pool.dma_start(type_w[:, 0, :], type_weights.partition_broadcast(P)).then_inc(consts_landed, 16)
            pool.dma_start(clip[:, 0, :], clips.partition_broadcast(P)).then_inc(consts_landed, 16)
            pool.dma_start(bias[:], bias_cols).then_inc(consts_landed, 16)
            step(pool.memset(ones[:], 1.0))
            step(pool.affine_select(out=ident[:], in_=ones[:], compare_op=ALU.is_equal, fill=0.0, base=0,
                                    pattern=[[-1, P]], channel_multiplier=1))
            pool.tensor_copy(ident_b[:], ident[:]).then_inc(ident_ready, 1)
            pool.wait_ge(ident_ready, 1)

            step(pool.memset(key_parts[:], -1))
            pool.dma_start(edge_i[:], edge_cols.rearrange("a p c -> p a c")).then_inc(edges_landed, 16)
            for a in range(2):
                pool.dma_start(key_parts[0:EC, a, 0:P], edge_rows[a]).then_inc(edges_landed, 16)
                pool.dma_start(key_parts[64:64 + EC, a, 0:SPAN], edge_rows[a][:, SPAN:P]).then_inc(edges_landed, 16)
            pool.dma_start(bo_all[:], bo.partition_broadcast(P)).then_inc(bo_landed, 16)
            step(pool.memset(dup[:], 0.0))
            step(pool.tensor_tensor(fold[:], ident_b[:, 0:EC], ident_b[:, 64:64 + EC], ALU.add))
            step(pool.iota(count[:], [[1, N]], base=0, channel_multiplier=0, allow_small_or_imprecise_dtypes=True))
            step(pool.iota(place[:], [[4, EC]], base=32, channel_multiplier=0))
            step(pool.memset(loops[:], 0.0))
            for m in range(NT):
                step(pool.tensor_copy(loops[:, m, m * P:(m + 1) * P], ident_b[:]))
            pool.tensor_scalar(loop_code[:], ident_b[:], 2.0 ** -96, 1.0, ALU.mult, ALU.mult).then_inc(edge_consts, 1)

            pool.wait_ge(norm_ready, NT)
            pool.wait_ge(bo_landed, 16)
            for m in range(NT):
                pool.tensor_tensor(rows[:, m, :], rows[:, m, :], bo_all[:], ALU.add).then_inc(residual_ready, 1)

            def ffn_integers(j):
                kind, t = FFN_JOBS[j]
                if j:
                    pool.wait_ge(ffn_rounded, j)
                if kind == "gate_up":
                    for g in range(2):
                        pool.dma_start(ffn_raw[:, g * F:(g + 1) * F], w_gate_up[2 * t + g]).then_inc(ffn_landed, 16)
                    width, tiles = F, 2
                else:
                    for g in range(2):
                        pool.dma_start(ffn_raw[:, 2 * g * I:(2 * g + 2) * I].rearrange("p (t i) -> p t i", t=2),
                                       w_down[4 * t + 2 * g:4 * t + 2 * g + 2].rearrange("t p i -> p t i")) \
                            .then_inc(ffn_landed, 16)
                    width, tiles = I, 4
                pool.wait_ge(ffn_scaled, j + 1)
                for g in range(tiles):
                    s = slice(g * width, (g + 1) * width)
                    step(pool.tensor_scalar(ffn_raw[:, s], ffn_raw[:, s], q_inv[:, g:g + 1], ROUND, ALU.mult, ALU.add))
                if j:
                    pool.wait_ge(ffn_turned, j)
                s = slice(0, tiles * width)
                pool.tensor_scalar(ffn_int[:, s], ffn_raw[:, s], -ROUND, 1.0, ALU.add, ALU.mult) \
                    .then_inc(ffn_rounded, 1)

            ffn_integers(0)
            ffn_integers(1)

            pool.wait_ge(classes_ready, 2 * NT)
            pool.wait_ge(type_w_ready, 1)
            for j in range(4):
                step(pool.tensor_scalar(picked[:], classes[:], float(j), type_w[:, 4, j:j + 1], ALU.is_equal, ALU.mult))
                last = pool.tensor_tensor(mask[:], mask[:], picked[:], ALU.add)
                if j < 3:
                    step(last)
            last.then_inc(mask_ready, 1)

            for j in range(2, len(FFN_JOBS)):
                ffn_integers(j)

            for h in range(HEADS):
                for m in range(NT):
                    pool.wait_ge(inv_ready, NT * h + m + 1)
                    pool.tensor_scalar(probs[h % 2][:, m, :], probs[h % 2][:, m, :], row_inv[:, h % 2, m:m + 1], 1.0,
                                       ALU.mult, ALU.mult).then_inc(probs_ready, 1)

            pool.wait_ge(scored, NT * HEADS)
            for t in range(KT):
                pool.tensor_scalar(diagonals[:, t * P:(t + 1) * P], ident[:], down_scale[:, t:t + 1], 1.0,
                                   ALU.mult, ALU.mult).then_inc(diagonals_ready, 1)

            for m in range(NT):
                for h in range(2):
                    s = slice(h * HALF, (h + 1) * HALF)
                    pool.wait_ge(ffn_out_ready, 2 * m + h + 1)
                    pool.tensor_tensor(rows[:, m, s], rows[:, m, s], ffn_out[:, m, s], ALU.add).then_inc(out_ready, 1)

        @block.tensor
        def _(pe):
            def three(out_ap, a_hi, a_lo, b_hi, b_lo, first, last):
                pe.matmul(out_ap, a_hi, b_hi, start=first, stop=False)
                pe.matmul(out_ap, a_hi, b_lo, start=False, stop=False)
                return pe.matmul(out_ap, a_lo, b_hi, start=False, stop=last)

            pe.sem_inc(unit_done, RING)
            pe.sem_inc(y_ready, RING)
            pe.sem_inc(hot_used, HOT_RING)

            pe.wait_ge(ident_ready, 1)
            for n in range(2 * NT):
                m, c = n // 2, n % 2
                pe.wait_ge(norm_ready, m + 1)
                if n >= 4:
                    pe.wait_ge(xT_ready, n - 3)
                for j in range(4):
                    k = 4 * c + j
                    mm = pe.transpose(bank[n % 4][:, j * P:(j + 1) * P], normed[:, m, k * P:(k + 1) * P], ident[:])
                mm.then_inc(norm_turned, 1)

            def project(p):
                src_hi, src_lo = (xT_hi, xT_lo) if p % 2 == 0 else (yT_hi, yT_lo)
                if p == 0:
                    pe.wait_ge(xT_ready, 2 * NT)
                with pe.Fori(0, GROUPS) as g:
                    for r in range(RING):
                        u = unit(p, g, r)
                        pe.wait_ge(lo_split, u + 1)
                        pe.wait_ge(y_ready, u + 1)
                        for k in range(KT):
                            if p % 2 and r == 0 and k > KT - RING:
                                pe.wait_ge(y_ready, (p - 1) * KT + k + 1 + RING)
                            s = slice(k * P, (k + 1) * P)
                            mm = three(bank[r][:, 0:N], w_hi[r][:, s], w_lo[r][:, s], src_hi[:, k, :], src_lo[:, k, :],
                                       k == 0, k == KT - 1)
                        mm.then_inc(unit_done, 1)

            def turn_ffn(j):
                kind, t = FFN_JOBS[j]
                pe.wait_ge(ffn_rounded, j + 1)
                if kind == "gate_up":
                    for g, b in enumerate((4, 7)):
                        if t == 0 and b == 7:
                            pe.wait_ge(classes_ready, 2)
                        into = bank[b][:].bitcast(BF16)
                        for k in range(KT):
                            mm = pe.transpose(into[:, k * P:(k + 1) * P],
                                              ffn_int[:, g * F + k * P:g * F + (k + 1) * P], ident_b[:])
                else:
                    for it in range(IT):
                        into = bank[4 if it < 2 else 7][:].bitcast(BF16)
                        w = min(P, I - it * P)
                        for q in range(4):
                            c = (4 * (it % 2) + q) * P
                            mm = pe.transpose(into[0:w, c:c + P], ffn_int[:, q * I + it * P:q * I + it * P + w],
                                              ident_b[:])
                mm.then_inc(ffn_turned, 1)

            project(0)

            pe.wait_ge(dup_ready, 2)
            pe.wait_ge(edge_consts, 1)
            pe.matmul(bank[4][:, 0:EC], dup[:], fold[:], start=True, stop=True).then_inc(dead_ready, 1)

            project(1)

            for m in range(NT):
                pe.matmul(bank[MASK_BANK[m]][:, 0:N], loop_code[:], loops[:, m, :], start=True, stop=False)

            def edge_chunk(r, last):
                for m in range(NT):
                    mm = pe.matmul(bank[MASK_BANK[m]][:, 0:N], src_hot[r][:, m * P:(m + 1) * P], dst_hot[r][:],
                                   start=False, stop=last)
                return mm

            with pe.Fori(0, EC // HOT_RING - 1) as g:
                for r in range(HOT_RING):
                    pe.wait_ge(hot_ready, g * HOT_RING + (r + 1))
                    edge_chunk(r, False).then_inc(hot_used, 1)
            for r in range(HOT_RING):
                pe.wait_ge(hot_ready, EC - HOT_RING + r + 1)
                mm = edge_chunk(r, r == HOT_RING - 1)
            mm.then_inc(mask_summed, 1)

            turn_ffn(0)
            project(2)
            pe.wait_ge(ffn_ready, 2)
            turn_ffn(1)
            project(3)
            pe.wait_ge(ffn_ready, 4)
            turn_ffn(2)
            project(4)
            pe.wait_ge(ffn_ready, 6)
            turn_ffn(3)

            pe.wait_ge(classes_ready, 2 * NT)
            for h in range(2):
                for r in range(RING):
                    pe.wait_ge(lo_split, unit(5, h, r) + 1)
                    for b in range(2):
                        k = 2 * r + b
                        if h == 0:
                            pe.wait_ge(y_ready, 4 * KT + k + 1 + RING)
                        s = slice(b * HALF, (b + 1) * HALF)
                        for m in range(NT):
                            n = slice(m * P, (m + 1) * P)
                            if h == 0 and k == 0 and m == 2:
                                pe.wait_ge(ffn_ready, 8)
                            mm = three(bank[V2_BANKS[h][m]][:], yT_hi[:, k, n], yT_lo[:, k, n],
                                       w_hi[r][:, s], w_lo[r][:, s], k == 0, k == KT - 1)
                            if k == KT - 1 and m < NT - 1:
                                mm.then_inc(v2_done, 1)
                    mm.then_inc(unit_done, 1)
            pe.wait_ge(v2_ready, NT)
            turn_ffn(4)

            def scores(h):
                a, c = slice(h % 2 * D, (h % 2 + 1) * D), h // 2
                for m in range(NT):
                    if h:
                        pe.wait_ge(scored, NT * (h - 1) + m + 1)
                    else:
                        pe.wait_ge(v2_ready, NT + m + 1)
                    n = slice(m * P, (m + 1) * P)
                    three(bank[m][:, 0:N], q2_hi[a, c, n], q2_lo[a, c, n], k2_hi[a, c, :], k2_lo[a, c, :],
                          True, True).then_inc(scores_done, 1)

            def turn_probs(h):
                if h:
                    pe.wait_ge(pT_ready, NT * h)
                else:
                    pe.wait_ge(ffn_ready, 10)
                for m in range(NT):
                    pe.wait_ge(probs_ready, NT * h + m + 1)
                    for c in range(NT):
                        mm = pe.transpose(bank[3 + c][:, m * P:(m + 1) * P], probs[h % 2][:, m, c * P:(c + 1) * P],
                                          ident[:])
                mm.then_inc(probs_turned, 1)

            def values(h):
                first = h // 2 * 2 * D
                width = D * (1 + h % 2)
                if h >= 2:
                    pe.wait_ge(o_ready, h - 1)
                for c in range(NT):
                    pe.wait_ge(pT_ready, NT * h + c + 1)
                    mm = three(bank[6 + h % 2][0:width, 0:N], v2_hi[:, c, first:first + width],
                               v2_lo[:, c, first:first + width], pT_hi[:, c, :], pT_lo[:, c, :], c == 0, c == NT - 1)
                mm.then_inc(values_done, 1)

            for i in range(HEADS + 2):
                if i < HEADS:
                    scores(i)
                if i >= 2:
                    values(i - 2)
                if 1 <= i <= HEADS:
                    turn_probs(i - 1)

            pe.wait_ge(scored, NT * HEADS)
            for r in range(RING):
                pe.wait_ge(lo_split, unit(6, 0, r) + 1)
                for b in range(2):
                    k = 2 * r + b
                    pe.wait_ge(o_ready, 2 * k + 2)
                    s = slice(b * HALF, (b + 1) * HALF)
                    for m in range(NT):
                        n = slice(m * P, (m + 1) * P)
                        mm = three(bank[m][:], yT_hi[:, k, n], yT_lo[:, k, n], w_hi[r][:, s], w_lo[r][:, s],
                                   k == 0, k == KT - 1)
                        if k == KT - 1 and m < NT - 1:
                            mm.then_inc(wo_done, 1)
                mm.then_inc(unit_done, 1)
            pe.wait_ge(o_ready, HEADS)
            pe.wait_ge(diagonals_ready, KT)
            for t in range(KT):
                mm = pe.matmul(bank[6 + t // 4][:, t % 4 * P:(t % 4 + 1) * P], ones[:], diagonals[:, t * P:(t + 1) * P],
                               start=True, stop=True)
            mm.then_inc(spread_done, 1)
            pe.wait_ge(pT_ready, NT * HEADS)
            for m in range(NT):
                n = slice(m * P, (m + 1) * P)
                for k in range(KT):
                    if m == 0 and k % 2 == 0:
                        pe.wait_ge(lo_split, unit(6, 1, k // 2) + 1)
                    s = slice(k % 2 * HALF, (k % 2 + 1) * HALF)
                    mm = three(bank[3 + m][:], yT_hi[:, k, n], yT_lo[:, k, n], w_hi[k // 2][:, s], w_lo[k // 2][:, s],
                               k == 0, k == KT - 1)
                mm.then_inc(wo_done, 1)

            def top_as_row(n):
                pe.wait_ge(top_ready, n + 1)
                pe.transpose(bank[7][0:1, 0:P], top[:, n:n + 1], ident[:]).then_inc(top_row, 1)

            def spread_top(n):
                pe.wait_ge(top_one, n + 1)
                pe.matmul(bank[6][:, n:n + 1], ones[0:1, :], top[0:1, 2 + n:3 + n], start=True, stop=True) \
                    .then_inc(top_all, 1)

            pe.wait_ge(spread_ready, 2)
            top_as_row(0)
            for m in range(NT):
                pe.wait_ge(norm2_ready, m + 1)
                for c in range(2):
                    for j in range(4):
                        k = 4 * c + j
                        mm = pe.transpose(bank[2 * m + c][:, j * P:(j + 1) * P], normed2[:, m, k * P:(k + 1) * P],
                                          ident[:])
                    mm.then_inc(norm2_turned, 1)
                if m == 0:
                    spread_top(0)

            pe.wait_ge(xq_ready, 2 * NT)
            for t in range(IT):
                for g in range(2):
                    for k in range(KT):
                        mm = pe.matmul(bank[2 * t + g][:, 0:N], gate_upT[:, k, g, t * P:(t + 1) * P], xqT[:, k, :],
                                       start=(k == 0), stop=(k == KT - 1))
                    mm.then_inc(gate_up_done, 1)
            top_as_row(1)
            spread_top(1)

            for m in range(NT):
                for h in range(2):
                    for t in range(IT):
                        if m == 0 and h == 0:
                            pe.wait_ge(hq_ready, t + 1)
                        w = min(P, I - t * P)
                        mm = pe.matmul(bank[2 * m + h][:], hqT[0:w, t, m * P:(m + 1) * P],
                                       downT[0:w, t, h * HALF:(h + 1) * HALF], start=(t == 0), stop=(t == IT - 1))
                    mm.then_inc(down_done, 1)

        @block.scalar
        def _(act):
            def head(p, g, r):
                n = (r + AHEAD) % RING
                groups = g + (p * GROUPS + (r + AHEAD) // RING)
                act.wait_ge(w_landed[n], groups * 16 + 16)
                act.wait_ge(unit_done, unit(p, g, r) + (AHEAD + 1))
                act.activation(w_hi[n][:], raw[n][:], ACT.Copy).then_inc(hi_split, 1)

            act.wait_ge(consts_landed, 48)
            act.activation(clip[:, 1, :], clip[:, 0, :], ACT.Exp, scale=-1.0).then_inc(softplus_exp, 1)
            act.activation(type_w[:, 1, :], type_w[:, 0, :], ACT.Abs).then_inc(act_step, 1)
            act.wait_ge(act_step, 1)
            act.activation(type_w[:, 2, :], type_w[:, 1, :], ACT.Exp, scale=-1.0).then_inc(act_step, 1)
            act.wait_ge(act_step, 2)
            act.activation(type_w[:, 3, :], type_w[:, 2, :], ACT.Ln, bias=1.0).then_inc(softplus_exp, 1)

            for u in range(AHEAD):
                act.wait_ge(w_landed[u], 16)
                act.activation(w_hi[u][:], raw[u][:], ACT.Copy).then_inc(hi_split, 1)

            for n in range(2 * NT):
                m, c = n // 2, n % 2
                act.wait_ge(norm_turned, n + 1)
                act.activation(xT_hi[:, 4 * c:4 * c + 4, m * P:(m + 1) * P],
                               bank[n % 4][:].rearrange("p (k n) -> p k n", k=4), ACT.Copy).then_inc(xT_hi_ready, 1)

            def project(p):
                dst = (yT_hi, q2_hi, yT_hi, k2_hi, yT_hi)[p]
                if p == 3:
                    act.wait_ge(mask_ready, 1)
                with act.Fori(0, GROUPS) as g:
                    for r in range(RING):
                        head(p, g, r)
                        act.wait_ge(unit_done, unit(p, g, r) + (1 + RING))
                        act.activation(dst[:, bass.ds(g * RING + r, 1), :].rearrange("p a n -> p (a n)"),
                                       bank[r][:, 0:N], ACT.Identity,
                                       bias=bias[:, p, bass.ds(g * RING + r, 1)]).then_inc(y_hi_ready, 1)

            def take_ffn(j):
                kind, t = FFN_JOBS[j]
                act.wait_ge(ffn_turned, j + 1)
                into = bank[4][:].bitcast(BF16)
                if kind == "gate_up":
                    ins = act.activation(gate_upT[:, :, 0, t * P:(t + 1) * P], into.rearrange("p (k i) -> p k i", k=KT),
                                         ACT.Copy)
                else:
                    ins = act.activation(downT[:, 0:2, 4 * t * P:4 * (t + 1) * P],
                                         into.rearrange("p (t f) -> p t f", t=2), ACT.Copy)
                ins.then_inc(ffn_ready, 1)

            project(0)
            project(1)
            for p in range(2, FEATURE_MAJOR):
                take_ffn(p - 2)
                project(p)
            take_ffn(3)

            for h in range(2):
                for r in range(RING):
                    head(5, h, r)
                for m in range(NT):
                    if m < NT - 1:
                        act.wait_ge(v2_done, 2 * h + m + 1)
                    else:
                        act.wait_ge(unit_done, unit(5, h, RING - 1) + 1 + RING)
                    act.activation(v2_hi[:, m, h * HALF:(h + 1) * HALF], bank[V2_BANKS[h][m]][:], ACT.Copy) \
                        .then_inc(v2_hi_ready, 1)
            take_ffn(4)
            head(6, 0, 0)
            head(6, 0, 1)

            def exponentials(h):
                b = h % 2
                for m in range(NT):
                    act.wait_ge(neg_ready, NT * h + m + 1)
                    act.activation(probs[b][:, m, :], probs[b][:, m, :], ACT.Exp, bias=neg_max[:, b, m:m + 1],
                                   scale=SCALE, accum_out=row_sum[:, b, m:m + 1]).then_inc(exp_ready, 1)

            def probs_head(h):
                act.wait_ge(probs_turned, h + 1)
                for c in range(NT):
                    act.activation(pT_hi[:, c, :], bank[3 + c][:, 0:N], ACT.Copy).then_inc(pT_hi_ready, 1)

            def output_head(h):
                a = slice(h % 2 * D, (h % 2 + 1) * D)
                act.wait_ge(values_done, h + 1)
                act.activation(yT_hi[a, h // 2, :], bank[6 + h % 2][a, 0:N], ACT.Identity,
                               bias=bias[a, 5, h // 2:h // 2 + 1]).then_inc(o_hi_ready, 1)

            for i in range(HEADS + 2):
                if i < HEADS:
                    exponentials(i)
                if i >= 2:
                    output_head(i - 2)
                if 1 <= i <= HEADS:
                    probs_head(i - 1)

            for r in range(2, RING + AHEAD):
                head(6, r // RING, r % RING)

            act.wait_ge(spread_done, 1)
            for b in range(2):
                act.activation(spread[:, b * HALF:(b + 1) * HALF], bank[6 + b][:], ACT.Copy).then_inc(spread_ready, 1)

            act.wait_ge(quant_ready, 1)
            for n in range(2 * NT):
                m, c = n // 2, n % 2
                act.wait_ge(norm2_turned, n + 1)
                act.activation(turned[:, 4 * c:4 * c + 4, m * P:(m + 1) * P],
                               bank[n][:].rearrange("p (k n) -> p k n", k=4), ACT.Identity, bias=top[:, 8:9],
                               scale=top[:, 6:7]).then_inc(x_rounded, 1)

            for t in range(IT):
                act.wait_ge(gate_up_done, 2 * t + 1)
                act.activation(gate_e[:, t, :], bank[2 * t][:, 0:N], ACT.Exp, scale=act_scale[:, 0, t:t + 1]) \
                    .then_inc(gate_exp, 1)

            act.wait_ge(quant_ready, 2)
            for t in range(IT):
                act.activation(hidden[:, t, :], hidden[:, t, :], ACT.Identity, bias=top[:, 8:9], scale=top[:, 7:8]) \
                    .then_inc(h_rounded, 1)

        @block.vector
        def _(dve):
            steps = [0]

            def step(ins):
                ins.then_inc(dve_step, 1)
                steps[0] += 1
                dve.wait_ge(dve_step, steps[0])

            def f32(ap):
                return ap.bitcast(F32)

            def tail(p, g, r):
                n = (r + AHEAD) % RING
                dve.wait_ge(hi_split, unit(p, g, r) + (AHEAD + 1))
                dve.tensor_tensor(w_lo[n][:], raw[n][:], f32(w_hi[n][:]), ALU.subtract).then_inc(lo_split, 1)

            def inverse_std(n):
                y, half_v, v, t = (newton[:, i, 0:n] for i in range(4))
                step(dve.tensor_scalar(v, mean_var[:, 0:n, 1], EPS, None, ALU.add))
                step(dve.tensor_scalar(bits[:, 0, 0:n], v.bitcast(I32), 1, None, ALU.logical_shift_right))
                step(dve.tensor_scalar(y.bitcast(I32), bits[:, 0, 0:n], -1.0, float(0x5F3759DF), ALU.mult, ALU.add))
                for _ in range(4):
                    step(dve.scalar_tensor_tensor(out=t, in0=y, scalar=-0.5, in1=y, op0=ALU.mult, op1=ALU.mult))
                    step(dve.tensor_tensor(half_v, t, v, ALU.mult))
                    step(dve.scalar_tensor_tensor(out=y, in0=half_v, scalar=1.5, in1=y, op0=ALU.add, op1=ALU.mult))

            for m in range(NT):
                dve.wait_ge(x_landed[m], 16)
                for h in range(2):
                    step(dve.bn_stats(stats[:, m, h, :], rows[:, m, h * HALF:(h + 1) * HALF]))
                step(dve.bn_aggr(mean_var[:, m, :], stats[:, m, :, :]))
            inverse_std(NT)
            for m in range(NT):
                dve.tensor_scalar(normed[:, m, :], rows[:, m, :], mean_var[:, m, 0:1], newton[:, 0, m:m + 1],
                                  ALU.subtract, ALU.mult).then_inc(norm_ready, 1)
            for u in range(AHEAD):
                dve.wait_ge(hi_split, u + 1)
                dve.tensor_tensor(w_lo[u][:], raw[u][:], f32(w_hi[u][:]), ALU.subtract).then_inc(lo_split, 1)
            for n in range(2 * NT):
                m, c = n // 2, n % 2
                dve.wait_ge(xT_hi_ready, n + 1)
                at = (slice(0, P), slice(4 * c, 4 * c + 4), slice(m * P, (m + 1) * P))
                dve.tensor_tensor(xT_lo[at], bank[n % 4][:].rearrange("p (k n) -> p k n", k=4), f32(xT_hi[at]),
                                  ALU.subtract).then_inc(xT_ready, 1)

            dve.wait_ge(edges_landed, 16 * 5)
            step(dve.scalar_tensor_tensor(out=keys[:], in0=key_parts[:, 0, :], scalar=float(N), in1=key_parts[:, 1, :],
                                          op0=ALU.mult, op1=ALU.add))
            dve.sem_inc(compared, 1)

            def project(p):
                dst_lo = (yT_lo, q2_lo, yT_lo, k2_lo, yT_lo)[p]
                dst_hi = (yT_hi, q2_hi, yT_hi, k2_hi, yT_hi)[p]
                with dve.Fori(0, GROUPS) as g:
                    for r in range(RING):
                        tail(p, g, r)
                        if p == 0:
                            find_doubles(g, r)
                        u = unit(p, g, r)
                        dve.wait_ge(y_hi_ready, u + 1)
                        c = bass.ds(g * RING + r, 1)
                        dve.scalar_tensor_tensor(out=dst_lo[:, c, :].rearrange("p a n -> p (a n)"), in0=bank[r][:, 0:N],
                                                 scalar=bias[:, p, c], in1=f32(dst_hi[:, c, :].rearrange("p a n -> p (a n)")),
                                                 op0=ALU.add, op1=ALU.subtract).then_inc(y_ready, 1)

            def find_doubles(g, r):
                w = SPAN // KT
                for e in range(w):
                    at = g * (RING * w) + (r * w + e)
                    dve.wait_ge(compared, at + 1)
                    dve.tensor_scalar(same[:], keys[:, bass.ds(at + 1, P - 1)], keys[:, bass.ds(at, 1)], None,
                                      ALU.is_equal, ALU.max, accum_out=overridden[:, bass.ds(at, 1)]) \
                        .then_inc(compared, 1)

            def ffn_scales(j):
                kind, t = FFN_JOBS[j]
                dve.wait_ge(ffn_landed, 32 * (j + 1))
                if kind == "gate_up":
                    view, scale = ffn_raw[:].rearrange("p (t f) -> p t f", t=2), gate_up_scale[:, t, :]
                else:
                    view = ffn_raw[:, 0:4 * I].rearrange("p (t i) -> p t i", t=4)
                    scale = down_scale[:, 4 * t:4 * t + 4]
                n = view.shape[1]
                step(dve.tensor_reduce(scale, view, AX.X, ALU.max, apply_absolute_value=True))
                step(dve.tensor_scalar(scale, scale, 1e-30, 1.0 / QMAX, ALU.max, ALU.mult))
                dve.reciprocal(q_inv[:, 0:n], scale).then_inc(ffn_scaled, 1)

            def take_ffn(j):
                kind, t = FFN_JOBS[j]
                dve.wait_ge(ffn_turned, j + 1)
                into = bank[7][:].bitcast(BF16)
                if kind == "gate_up":
                    ins = dve.tensor_copy(gate_upT[:, :, 1, t * P:(t + 1) * P], into.rearrange("p (k i) -> p k i", k=KT))
                else:
                    w = I - 2 * P
                    ins = dve.tensor_copy(downT[0:w, 2, 4 * t * P:4 * (t + 1) * P], into[0:w, 0:4 * P])
                ins.then_inc(ffn_ready, 1)

            project(0)
            dve.wait_ge(compared, SPAN + 1)
            dve.wait_ge(edge_consts, 1)
            dve.tensor_copy(dup[0:EC, 0:SPAN], overridden[0:EC, :]).then_inc(dup_ready, 1)
            dve.tensor_copy(dup[64:64 + EC, SPAN:P], overridden[64:64 + EC, :]).then_inc(dup_ready, 1)
            ffn_scales(0)
            step(dve.tensor_copy(edge_f[:], edge_i[:]))
            kinds = edge_f[:, 2, :]
            for v, c in ((1.0, 1.0), (2.0, 2.0), (3.0, 4.0)):
                to = code[:, 0, :] if v == 1.0 else code[:, 1, :]
                step(dve.tensor_scalar(to, kinds, v, c, ALU.is_equal, ALU.mult))
                if v != 1.0:
                    step(dve.tensor_tensor(code[:, 0, :], code[:, 0, :], to, ALU.add))
            for v, o in ((4.0, ALU.is_ge), (0.0, ALU.is_equal)):
                step(dve.tensor_scalar(code[:, 1, :], kinds, v, 8.0, o, ALU.mult))
                step(dve.tensor_tensor(code[:, 0, :], code[:, 0, :], code[:, 1, :], ALU.add))
            step(dve.tensor_scalar(place[:], place[:], 23, None, ALU.logical_shift_left))
            step(dve.tensor_tensor(code[:, 0, :], code[:, 0, :], place[:].bitcast(F32), ALU.mult))
            dve.wait_ge(dead_ready, 1)
            step(dve.tensor_scalar(code[:, 1, :], bank[4][:, 0:EC], -1.0, 1.0, ALU.mult, ALU.add))
            step(dve.tensor_tensor(code[:, 2, :], code[:, 0, :], code[:, 1, :], ALU.mult))
            project(1)
            ffn_scales(1)

            def one_hots(g, r):
                c = bass.ds(g * HOT_RING + r, 1)
                dve.wait_ge(hot_used, g * HOT_RING + (r + 1))
                dve.tensor_scalar(src_hot[r][:], count[:], edge_f[:, 0, c], code[:, 2, c], ALU.is_equal, ALU.mult)
                dve.tensor_scalar(dst_hot[r][:], count[:], edge_f[:, 1, c], None, ALU.is_equal).then_inc(hot_ready, 1)

            with dve.Fori(0, EC // HOT_RING) as g:
                for r in range(HOT_RING):
                    one_hots(g, r)

            dve.wait_ge(mask_summed, 1)
            for m in range(NT):
                sums = bank[MASK_BANK[m]][:, 0:N]
                dve.tensor_scalar(classes[:, m, :], sums.bitcast(I32), 23, 3, ALU.logical_shift_right,
                                  ALU.bitwise_and).then_inc(classes_ready, 1)
                dve.tensor_scalar(mask[:, m, :], sums, 0.0, NO_EDGE, ALU.is_equal, ALU.mult).then_inc(classes_ready, 1)
            dve.wait_ge(softplus_exp, 2)
            step(dve.tensor_scalar(type_w[:, 4, :], type_w[:, 0, :], 0.0, None, ALU.max))
            step(dve.tensor_tensor(type_w[:, 4, :], type_w[:, 4, :], type_w[:, 3, :], ALU.add))
            dve.tensor_scalar(type_w[:, 4, :], type_w[:, 4, :], 1.0 / SCALE, None, ALU.mult).then_inc(type_w_ready, 1)
            step(dve.tensor_scalar(clip[:, 2, :], clip[:, 1, :], 1.0, None, ALU.add))
            step(dve.reciprocal(clip[:, 3, :], clip[:, 2, :]))
            step(dve.memset(top[:, 8:9], ROUND))

            take_ffn(0)
            project(2)
            take_ffn(1)
            ffn_scales(2)
            dve.wait_ge(mask_ready, 1)
            project(3)
            take_ffn(2)
            ffn_scales(3)
            project(4)
            take_ffn(3)
            ffn_scales(4)

            for h in range(2):
                for r in range(RING):
                    tail(5, h, r)
                for m in range(NT):
                    s = slice(h * HALF, (h + 1) * HALF)
                    dve.wait_ge(v2_hi_ready, NT * h + m + 1)
                    dve.tensor_tensor(v2_lo[:, m, s], bank[V2_BANKS[h][m]][:], f32(v2_hi[:, m, s]), ALU.subtract) \
                        .then_inc(v2_ready, 1)
            take_ffn(4)
            tail(6, 0, 0)
            tail(6, 0, 1)

            def masked_max(h):
                b = h % 2
                for m in range(NT):
                    dve.wait_ge(scores_done, NT * h + m + 1)
                    if h >= 2:
                        dve.wait_ge(probs_turned, h - 1)
                    dve.tensor_tensor_reduce(out=probs[b][:, m, :], in0=bank[m][:, 0:N], in1=mask[:, m, :],
                                             scale=1.0, scalar=-3.0e38, op0=ALU.add, op1=ALU.max,
                                             accum_out=row_max[:, b, m:m + 1]).then_inc(scored, 1)
                    dve.wait_ge(scored, NT * h + m + 1)
                    dve.tensor_scalar(neg_max[:, b, m:m + 1], row_max[:, b, m:m + 1], -SCALE, None,
                                      ALU.mult).then_inc(neg_ready, 1)

            def inverse_sums(h):
                b = h % 2
                for m in range(NT):
                    dve.wait_ge(exp_ready, NT * h + m + 1)
                    dve.reciprocal(row_inv[:, b, m:m + 1], row_sum[:, b, m:m + 1]).then_inc(inv_ready, 1)

            def probs_tail(h):
                for c in range(NT):
                    dve.wait_ge(pT_hi_ready, NT * h + c + 1)
                    dve.tensor_tensor(pT_lo[:, c, :], bank[3 + c][:, 0:N], f32(pT_hi[:, c, :]), ALU.subtract) \
                        .then_inc(pT_ready, 1)

            def output_tail(h):
                a = slice(h % 2 * D, (h % 2 + 1) * D)
                dve.wait_ge(o_hi_ready, h + 1)
                dve.scalar_tensor_tensor(out=yT_lo[a, h // 2, :], in0=bank[6 + h % 2][a, 0:N],
                                         scalar=bias[a, 5, h // 2:h // 2 + 1], in1=f32(yT_hi[a, h // 2, :]),
                                         op0=ALU.add, op1=ALU.subtract).then_inc(o_ready, 1)

            for i in range(HEADS + 2):
                if i < HEADS:
                    masked_max(i)
                    inverse_sums(i)
                if i >= 2:
                    output_tail(i - 2)
                if 1 <= i <= HEADS:
                    probs_tail(i - 1)

            for r in range(2, RING + AHEAD):
                tail(6, r // RING, r % RING)

            for h in range(2):
                for m in range(NT):
                    s = slice(h * HALF, (h + 1) * HALF)
                    if h == 0 and m == NT - 1:
                        dve.wait_ge(unit_done, unit(6, 0, RING - 1) + 1 + RING)
                    else:
                        dve.wait_ge(wo_done, (NT - 1) * h + m + 1)
                    dve.wait_ge(residual_ready, NT)
                    step(dve.tensor_tensor(rows[:, m, s], bank[3 * h + m][:], rows[:, m, s], ALU.add))
                    dve.bn_stats(stats[:, m, h, :], rows[:, m, s])
                    dve.tensor_reduce(extremes[:, 0, m, h:h + 1], rows[:, m, s], AX.X, ALU.max)
                    step(dve.tensor_reduce(extremes[:, 1, m, h:h + 1], rows[:, m, s], AX.X, ALU.min))
            for m in range(NT):
                step(dve.bn_aggr(mean_var[:, m, :], stats[:, m, :, :]))
            inverse_std(NT)
            for i, op in enumerate((ALU.max, ALU.min)):
                e = newton[:, 2 + i, :]
                step(dve.tensor_tensor(e, extremes[:, i, :, 0], extremes[:, i, :, 1], op))
                step(dve.tensor_tensor(e, e, mean_var[:, :, 0], ALU.subtract))
                step(dve.tensor_tensor(e, e, newton[:, 0, :], ALU.mult))
            dve.tensor_reduce(top[:, 0:1], newton[:, 2:4, :].rearrange("p a b -> p (a b)"), AX.X, ALU.max, apply_absolute_value=True) \
                .then_inc(top_ready, 1)

            def normalise(m):
                dve.tensor_scalar(normed2[:, m, :], rows[:, m, :], mean_var[:, m, 0:1], newton[:, 0, m:m + 1],
                                  ALU.subtract, ALU.mult).then_inc(norm2_ready, 1)

            def top_of_row(n):
                dve.wait_ge(top_row, n + 1)
                dve.tensor_reduce(top[0:1, 2 + n:3 + n], bank[7][0:1, 0:P], AX.X, ALU.max).then_inc(top_one, 1)

            def scale_from_top(n):
                dve.wait_ge(top_all, n + 1)
                step(dve.tensor_scalar(top[:, 4 + n:5 + n], bank[6][:, n:n + 1], clip[:, 3, n:n + 1], 1.0 / QMAX,
                                       ALU.mult, ALU.mult))
                dve.reciprocal(top[:, 6 + n:7 + n], top[:, 4 + n:5 + n]).then_inc(quant_ready, 1)

            def clip_rounded(rounded, integers, ready):
                step(dve.tensor_scalar(rounded, rounded, ROUND + QMAX, ROUND - QMAX - 1.0, ALU.min, ALU.max))
                dve.tensor_scalar(integers, rounded, -ROUND, None, ALU.add).then_inc(ready, 1)

            normalise(0)
            top_of_row(0)
            normalise(1)
            scale_from_top(0)
            normalise(2)
            for i, (g, sign) in enumerate(((0, -1.0), (0, 1.0), (1, 1.0))):
                ins = dve.tensor_scalar(act_scale[:, i, :], gate_up_scale[:, :, g], top[:, 4:5], sign,
                                        ALU.mult, ALU.mult)
            step(ins)
            for n in range(2 * NT):
                m, c = n // 2, n % 2
                at = (slice(0, P), slice(4 * c, 4 * c + 4), slice(m * P, (m + 1) * P))
                dve.wait_ge(x_rounded, n + 1)
                clip_rounded(turned[at], xqT[at], xq_ready)

            for t in range(IT):
                dve.wait_ge(gate_exp, t + 1)
                step(dve.tensor_scalar(gate_s[:, t, :], gate_e[:, t, :], 1.0, None, ALU.add))
                step(dve.reciprocal(gate_s[:, t, :], gate_s[:, t, :]))
                step(dve.scalar_tensor_tensor(out=gate_s[:, t, :], in0=bank[2 * t][:, 0:N], scalar=act_scale[:, 1, t:t + 1],
                                              in1=gate_s[:, t, :], op0=ALU.mult, op1=ALU.mult))
                dve.wait_ge(gate_up_done, 2 * t + 2)
                step(dve.scalar_tensor_tensor(out=hidden[:, t, :], in0=bank[2 * t + 1][:, 0:N],
                                              scalar=act_scale[:, 2, t:t + 1], in1=gate_s[:, t, :],
                                              op0=ALU.mult, op1=ALU.mult))
                step(dve.tensor_reduce(top[:, 10 + t:11 + t], hidden[:, t, :], AX.X, ALU.max, apply_absolute_value=True))
            dve.tensor_reduce(top[:, 1:2], top[:, 10:10 + IT], AX.X, ALU.max).then_inc(top_ready, 1)
            top_of_row(1)
            scale_from_top(1)
            for t in range(IT):
                dve.wait_ge(h_rounded, t + 1)
                clip_rounded(hidden[:, t, :], hqT[:, t, :], hq_ready)

            for m in range(NT):
                for h in range(2):
                    s = slice(h * HALF, (h + 1) * HALF)
                    dve.wait_ge(down_done, 2 * m + h + 1)
                    dve.scalar_tensor_tensor(out=ffn_out[:, m, s], in0=bank[2 * m + h][:], scalar=top[:, 5:6],
                                             in1=spread[:, s], op0=ALU.mult, op1=ALU.mult).then_inc(ffn_out_ready, 1)


def kernel(x, src, dst, edge_type_5, L0_gnn_edge_type_weights, L0_gnn_wq, L0_gnn_bq, L0_gnn_wk, L0_gnn_bk, L0_gnn_wv,
           L0_gnn_bv, L0_gnn_wiq, L0_gnn_biq, L0_gnn_wik, L0_gnn_bik, L0_gnn_wiv, L0_gnn_biv, L0_gnn_wo, L0_gnn_bo,
           L0_ffn_clip_x, L0_ffn_clip_down, L0_ffn_w_gate, L0_ffn_w_up, L0_ffn_w_down):
    import numpy as np
    import concourse.bacc as bacc
    from concourse.bass_utils import run_bass_kernel_spmd

    N, F = x.shape
    KT = F // P
    EC = src.shape[0] // P

    def block_units(w):
        return np.asarray(w).reshape(KT, P, KT, P).transpose(0, 3, 2, 1).reshape(KT, P, F)

    def half_units(w):
        return np.asarray(w).reshape(2, F // 2, KT // 2, 2, P).transpose(0, 2, 4, 3, 1).reshape(KT, P, F)

    def row_tiles(w):
        w = np.asarray(w)
        tiles = -(-w.shape[0] // P)
        return np.pad(w, ((0, tiles * P - w.shape[0]), (0, 0))).reshape(tiles, P, w.shape[1])

    weights = np.concatenate([block_units(w) for w in (L0_gnn_wq, L0_gnn_wiq, L0_gnn_wk, L0_gnn_wik, L0_gnn_wv)]
                             + [half_units(w) for w in (L0_gnn_wiv, L0_gnn_wo)])
    biases = (L0_gnn_bq, L0_gnn_biq, L0_gnn_bk, L0_gnn_bik, L0_gnn_bv, L0_gnn_biv)
    edges = [np.asarray(e).reshape(EC, P) for e in (src, dst, edge_type_5)]
    gate, up = row_tiles(L0_ffn_w_gate), row_tiles(L0_ffn_w_up)
    arrays = {
        "x_rows": np.asarray(x),
        "weights": weights,
        "bias_cols": np.stack([np.asarray(b).reshape(KT, P).T for b in biases], 1),
        "bo": np.asarray(L0_gnn_bo),
        "edge_cols": np.stack([e.T for e in edges]),
        "edge_rows": np.stack(edges[:2]),
        "type_weights": np.asarray(L0_gnn_edge_type_weights),
        "clips": np.concatenate([np.asarray(L0_ffn_clip_x), np.asarray(L0_ffn_clip_down)]),
        "w_gate_up": np.stack([gate, up], 1).reshape(2 * gate.shape[0], P, F),
        "w_down": row_tiles(L0_ffn_w_down),
    }
    arrays = {name: np.ascontiguousarray(a) for name, a in arrays.items()}
    nc = bacc.Bacc("TRN2", target_bir_lowering=False, num_devices=1)
    args = [nc.dram_tensor(name, a.shape, mybir.dt.from_np(a.dtype), kind="ExternalInput").ap()
            for name, a in arrays.items()]
    out = nc.dram_tensor("out_rows", (N, F), F32, kind="ExternalOutput").ap()
    gnn_ffn(nc, *args, out)
    result = run_bass_kernel_spmd(nc, [arrays], core_ids=[0])
    return result.results[0]["out_rows"]
```

```python
from contextlib import ExitStack

import concourse.bass as bass
from concourse import mybir

P = 128
ALU = mybir.AluOpType
ACT = mybir.ActivationFunctionType
AX = mybir.AxisListType
F32 = mybir.dt.float32
F32R = mybir.dt.float32r
BF16 = mybir.dt.bfloat16
F16 = mybir.dt.float16
I32 = mybir.dt.int32

RING = 4
AHEAD = 2
LAYERS = 4
ROUND = 1.5 * 2.0 ** 23
QMAX = 127.0
NO_EDGE = -1.0e30
EPS = 1e-5
HEADS = 16
FEATURE_MAJOR = 5
FFN_JOBS = [("gate_up", 0), ("gate_up", 1), ("gate_up", 2), ("down", 0), ("down", 1)]


def gnn_ffn(nc, x, weights, bias_cols, bo, edge_cols, edge_rows, type_weights, clips, w_gate_up, w_down, layers, out):
    N, F = x.shape
    NT = N // P
    KT = F // P
    HALF = F // 2
    D = F // HEADS
    EC = edge_cols.shape[2]
    SPAN = P // 2
    IT = w_gate_up.shape[0] // 2
    I = w_down.shape[2]
    SCALE = float(D) ** -0.5
    UNITS = weights.shape[0]
    GROUPS = KT // RING
    assert NT == 3 and KT == 8 and D == 64 and UNITS == 7 * KT and IT * P <= N
    assert EC % (2 * LAYERS) == 0 and EC <= 64 and 4 * (EC + 1) < 2 ** 20

    with ExitStack() as ctx:
        def sb(name, shape, dt, stack=ctx):
            return stack.enter_context(nc.sbuf_tensor(name, shape, dt))

        def sem(name):
            return ctx.enter_context(nc.semaphore(name))

        bank = [ctx.enter_context(nc.psum_tensor(f"bank{b}", [P, 512], F32)) for b in range(8)]

        rows = sb("rows", [P, NT, F], F32)
        raw = [sb(f"raw{r}", [P, F], F32) for r in range(RING)]
        w_hi = [sb(f"w_hi{r}", [P, F], F32R) for r in range(RING)]
        w_lo = [sb(f"w_lo{r}", [P, F], F32R) for r in range(RING)]
        mask = sb("mask", [P, NT, N], F32)
        gate_upT = sb("gate_upT", [P, KT, 2, IT * P], BF16)
        with ExitStack() as early:
            classes = sb("classes", [P, NT, N], F32, early)
        downT = sb("downT", [P, IT, F], BF16)
        ident = sb("ident", [P, P], F32)
        ident_b = sb("ident_b", [P, P], BF16)
        ones = sb("ones", [P, P], F32)
        bias = sb("bias", [P, 6, KT], F32)
        bo_all = sb("bo_all", [P, F], F32)
        stats = sb("stats", [P, NT, 2, 6], F32)
        mean_var = sb("mean_var", [P, NT, 2], F32)
        newton = sb("newton", [P, 6, NT], F32)
        neg_max = sb("neg_max", [P, 2, NT], F32)
        row_sum = sb("row_sum", [P, 2, NT], F32)
        row_inv = sb("row_inv", [P, 2, NT], F32)
        type_w = sb("type_w", [P, 5, 4], F32)
        clip = sb("clip", [P, 4, 2], F32)
        gate_up_scale = sb("gate_up_scale", [P, IT, 2], F32)
        down_scale = sb("down_scale", [P, KT], F32)
        q_inv = sb("q_inv", [P, 4], F32)
        extremes = sb("extremes", [P, NT, 2, 2], F32)
        top = sb("top", [P, 24], F32)
        act_scale = sb("act_scale", [P, 2, IT], F32)
        cell_value = sb("cell_value", [P, 2, EC], I32)
        staged = [sb(f"staged{b}", [P, 2, LAYERS], I32) for b in range(2)]

        with ExitStack() as early:
            key_parts = sb("key_parts", [P, 2, 192], I32, early)
            keys = sb("keys", [P, 192], F32, early)
            same = sb("same", [P, SPAN // KT, P - 1], BF16, early)
            overridden = sb("overridden", [P, SPAN], BF16, early)
            edge_i = sb("edge_i", [P, 3, EC], I32, early)
            edge_f = sb("edge_f", [P, 3, EC], F32, early)
            edge_value = sb("edge_value", [P, 3, EC], F32, early)
            edge_cell = sb("edge_cell", [P, EC], F32, early)
            alive = sb("alive", [P, EC], F32, early)
            spare_cell = sb("spare_cell", [P, 1], F32, early)
        with ExitStack() as late:
            turned = sb("turned", [P, KT, N], F32, late)
            xqT = sb("xqT", [P, KT, N], BF16, late)
            gate_s = sb("gate_s", [P, IT, N], F32, late)
            hidden = sb("hidden", [P, IT, N], F32, late)
            hqT = sb("hqT", [P, IT, N], BF16, late)
            diagonals = sb("diagonals", [P, F], F32, late)
            spread = sb("spread", [P, F], F32, late)
        k2_hi = sb("k2_hi", [P, KT, N], F32R)
        k2_lo = sb("k2_lo", [P, KT, N], F32R)
        q2_hi = sb("q2_hi", [P, KT, N], F32R)
        q2_lo = sb("q2_lo", [P, KT, N], F32R)

        with ExitStack() as late:
            normed2 = sb("normed2", [P, NT, F], F32, late)
            ffn_out = sb("ffn_out", [P, NT, F], F32, late)
        xT_hi = sb("xT_hi", [P, KT, N], F32R)
        xT_lo = sb("xT_lo", [P, KT, N], F32R)
        v2_hi = xT_hi[:].rearrange("p a b -> p (a b)").rearrange("p (m f) -> p m f", m=NT)
        v2_lo = xT_lo[:].rearrange("p a b -> p (a b)").rearrange("p (m f) -> p m f", m=NT)

        with ExitStack() as early:
            normed = sb("normed", [P, NT, F], F32, early)
        yT_hi = sb("yT_hi", [P, KT, N], F32R)
        yT_lo = sb("yT_lo", [P, KT, N], F32R)

        with ExitStack() as early:
            picked = [sb(f"picked{b}", [P, NT, N], F32, early) for b in range(2)]
            ffn_raw = sb("ffn_raw", [P, 2 * F], F32, early)
            ffn_int = sb("ffn_int", [P, 2 * F], BF16, early)
        probs = [sb(f"probs{b}", [P, NT, N], F32) for b in range(2)]
        pT_hi = sb("pT_hi", [P, NT, N], F32R)
        pT_lo = sb("pT_lo", [P, NT, N], F32R)

        x_landed = [sem(f"x_landed{m}") for m in range(NT)]
        consts_landed = sem("consts_landed")
        edges_landed = sem("edges_landed")
        bo_landed = sem("bo_landed")
        w_landed = [sem(f"w_landed{r}") for r in range(RING)]
        ffn_landed = sem("ffn_landed")
        ident_ready = sem("ident_ready")
        dve_step = sem("dve_step")
        act_step = sem("act_step")
        pool_step = sem("pool_step")
        compared = sem("compared")
        dead_ready = sem("dead_ready")
        blank_ready = sem("blank_ready")
        edge_consts = sem("edge_consts")
        layers_cleared = sem("layers_cleared")
        cells_ready = sem("cells_ready")
        edges_staged = sem("edges_staged")
        chunk_turn = sem("chunk_turn")
        written = [sem(f"written{g}") for g in range(LAYERS)]
        layers_landed = sem("layers_landed")
        picked_ready = sem("picked_ready")
        picked_used = sem("picked_used")
        keys_cleared = sem("keys_cleared")
        softplus_exp = sem("softplus_exp")
        mask_ready = sem("mask_ready")
        var_ready = sem("var_ready")
        root_ready = sem("root_ready")
        std_ready = sem("std_ready")
        norm_ready = sem("norm_ready")
        norm_last_ready = sem("norm_last_ready")
        norm_turned = sem("norm_turned")
        xT_hi_ready = sem("xT_hi_ready")
        xT_ready = sem("xT_ready")
        hi_split = sem("hi_split")
        lo_split = sem("lo_split")
        unit_done = sem("unit_done")
        y_hi_ready = sem("y_hi_ready")
        y_ready = sem("y_ready")
        ffn_scaled = sem("ffn_scaled")
        ffn_rounded = sem("ffn_rounded")
        ffn_turned = sem("ffn_turned")
        ffn_ready = sem("ffn_ready")
        v2_done = sem("v2_done")
        v2_hi_ready = sem("v2_hi_ready")
        v2_ready = sem("v2_ready")
        scores_done = sem("scores_done")
        scored = sem("scored")
        exp_ready = sem("exp_ready")
        inv_ready = sem("inv_ready")
        probs_ready = sem("probs_ready")
        probs_turned = sem("probs_turned")
        pT_hi_ready = sem("pT_hi_ready")
        pT_ready = sem("pT_ready")
        values_done = sem("values_done")
        o_hi_ready = sem("o_hi_ready")
        o_ready = sem("o_ready")
        residual_ready = sem("residual_ready")
        wo_done = sem("wo_done")
        norm2_ready = sem("norm2_ready")
        norm2_turned = sem("norm2_turned")
        top_ready = sem("top_ready")
        top_row = sem("top_row")
        top_one = sem("top_one")
        top_all = sem("top_all")
        quant_ready = sem("quant_ready")
        x_rounded = sem("x_rounded")
        x_clipped = sem("x_clipped")
        xq_ready = sem("xq_ready")
        gate_up_done = sem("gate_up_done")
        gate_sigmoid = sem("gate_sigmoid")
        hq_ready = sem("hq_ready")
        down_done = sem("down_done")
        diagonals_ready = sem("diagonals_ready")
        spread_done = sem("spread_done")
        spread_ready = sem("spread_ready")
        ffn_out_ready = sem("ffn_out_ready")
        out_first = sem("out_first")
        out_second = sem("out_second")
        stored = sem("stored")

        WO_TAILS = (3, 7)
        layer_rows = (mask, classes, picked[0], picked[1])
        GATE_UP_BANKS = ((0, 1, 2), (3, 4, 5))
        TURN_ORDER = (0, 1, 3, 4, 2, 5)
        V2_BANKS = ((0, 1, 2), (5, 6, 3))

        def piece(n):
            c, m = n // NT, n % NT
            return slice(0, P), slice(4 * c, 4 * c + 4), slice(m * P, (m + 1) * P)

        def unit(p, g, r):
            return g * RING + (p * KT + r)

        block = ctx.enter_context(nc.Block())

        @block.sync
        def _(sp):
            for m in range(NT):
                sp.dma_start(rows[:, m, :], x.rearrange("(m p) f -> p m f", p=P)[:, m, :]).then_inc(x_landed[m], 16)
            for r in range(RING):
                sp.dma_start(raw[r][:], weights[r]).then_inc(w_landed[r], 16)
            sp.dma_start(edge_i[:], edge_cols.rearrange("a p c -> p a c")).then_inc(edges_landed, 16)
            sp.wait_ge(keys_cleared, 1)
            for a in range(2):
                sp.dma_start(key_parts[0:EC, a, 0:P], edge_rows[a]).then_inc(edges_landed, 16)
                sp.dma_start(key_parts[64:64 + EC, a, 0:SPAN], edge_rows[a][:, SPAN:P]).then_inc(edges_landed, 16)
            with sp.Fori(1, UNITS // RING) as g:
                for r in range(RING):
                    sp.wait_ge(hi_split, g * RING + (r + 1 - RING))
                    sp.wait_ge(lo_split, g * RING + (r + 1 - RING))
                    sp.dma_start(raw[r][:], weights[bass.ds(g * RING + r, 1)].rearrange("a p f -> (a p) f")) \
                        .then_inc(w_landed[r], 16)
            for m in range(NT):
                for h in range(2):
                    s = slice(h * HALF, (h + 1) * HALF)
                    sp.wait_ge((out_first, out_second)[h], m + 1)
                    sp.dma_start(out.rearrange("(m p) f -> p m f", p=P)[:, m, s], rows[:, m, s]).then_inc(stored, 16)
            sp.wait_ge(stored, 16 * NT * 2)

        @block.gpsimd
        def _(pool):
            steps = [0]

            def step(ins):
                ins.then_inc(pool_step, 1)
                steps[0] += 1
                pool.wait_ge(pool_step, steps[0])

            step(pool.memset(ones[:], 1.0))
            step(pool.affine_select(out=ident[:], in_=ones[:], compare_op=ALU.is_equal, fill=0.0, base=0,
                                    pattern=[[-1, P]], channel_multiplier=1))
            pool.tensor_copy(ident_b[:], ident[:]).then_inc(ident_ready, 1)
            pool.memset(key_parts[:], -1).then_inc(keys_cleared, 1)
            pool.dma_start(type_w[:, 0, :], type_weights.partition_broadcast(P)).then_inc(consts_landed, 16)
            pool.dma_start(clip[:, 0, :], clips.partition_broadcast(P)).then_inc(consts_landed, 16)
            pool.dma_start(bias[:], bias_cols).then_inc(consts_landed, 16)
            pool.memset(picked[0][:], 0.0).then_inc(blank_ready, 1)
            step(pool.memset(mask[:], 0.0))
            pool.wait_ge(ident_ready, 1)
            for m in range(NT):
                pool.tensor_scalar(mask[:, m, m * P:(m + 1) * P], ident[:], 3.0, 1.0, ALU.mult, ALU.mult) \
                    .then_inc(blank_ready, 1)
            step(pool.iota(edge_value[:, 2, :], [[4, EC]], base=4, channel_multiplier=0,
                           allow_small_or_imprecise_dtypes=True))
            step(pool.iota(spare_cell[:], [[0, 1]], base=0, channel_multiplier=1, allow_small_or_imprecise_dtypes=True))
            pool.tensor_scalar(spare_cell[:], spare_cell[:], float(N * N), 1.0, ALU.add, ALU.mult).then_inc(edge_consts, 1)
            for u in range(AHEAD):
                pool.wait_ge(hi_split, u + 1)
                pool.tensor_tensor(w_lo[u][:], raw[u][:], w_hi[u][:].bitcast(F32), ALU.subtract).then_inc(lo_split, 1)
            pool.dma_start(bo_all[:], bo.partition_broadcast(P)).then_inc(bo_landed, 16)

            def load_ffn(j):
                kind, t = FFN_JOBS[j]
                if j:
                    pool.wait_ge(ffn_rounded, j)
                if kind == "gate_up":
                    for g in range(2):
                        pool.dma_start(ffn_raw[:, g * F:(g + 1) * F], w_gate_up[2 * t + g]).then_inc(ffn_landed, 16)
                else:
                    for g in range(2):
                        pool.dma_start(ffn_raw[:, 2 * g * I:(2 * g + 2) * I].rearrange("p (t i) -> p t i", t=2),
                                       w_down[4 * t + 2 * g:4 * t + 2 * g + 2].rearrange("t p i -> p t i")) \
                            .then_inc(ffn_landed, 16)

            def ffn_integers(j):
                width, tiles = (F, 2) if FFN_JOBS[j][0] == "gate_up" else (I, 4)
                pool.wait_ge(ffn_scaled, j + 1)
                for g in range(tiles):
                    s = slice(g * width, (g + 1) * width)
                    step(pool.tensor_scalar(ffn_raw[:, s], ffn_raw[:, s], q_inv[:, g:g + 1], ROUND, ALU.mult, ALU.add))
                if j:
                    pool.wait_ge(ffn_turned, j)
                s = slice(0, tiles * width)
                pool.tensor_scalar(ffn_int[:, s], ffn_raw[:, s], -ROUND, 1.0, ALU.add, ALU.mult) \
                    .then_inc(ffn_rounded, 1)

            def tail(p, g, r):
                n = (r + AHEAD) % RING
                pool.wait_ge(hi_split, unit(p, g, r) + (AHEAD + 1))
                pool.tensor_tensor(w_lo[n][:], raw[n][:], w_hi[n][:].bitcast(F32), ALU.subtract).then_inc(lo_split, 1)

            load_ffn(0)
            with pool.Fori(0, GROUPS) as g:
                for r in range(RING):
                    tail(0, g, r)
            ffn_integers(0)
            load_ffn(1)

            pool.wait_ge(cells_ready, 1)
            pool.wait_ge(layers_cleared, 16 * LAYERS)
            pool.sem_inc(edges_staged, 1)

            def write_chunks(i, first):
                for b in range(2):
                    pool.tensor_copy(staged[b][:], cell_value[:, :, bass.ds(i * (2 * LAYERS) + b * LAYERS, LAYERS)]) \
                        .then_inc(edges_staged, 1)
                    pool.wait_ge(edges_staged, i * 2 + b + 2)
                    for g in range(LAYERS):
                        if b or not first:
                            pool.wait_ge(written[g], (i * 2 + b) * 16)
                        pool.sem_inc(chunk_turn, 1)
                        pool.indirect_dma_start(layers[g], bass.IndirectOffsetOnAxis(ap=staged[b][:, 0, g:g + 1], axis=0),
                                                staged[b][:, 1, g:g + 1], None).then_inc(written[g], 16)

            write_chunks(0, True)
            with pool.Fori(1, EC // (2 * LAYERS)) as i:
                write_chunks(i, False)
            for g in range(LAYERS):
                pool.wait_ge(written[g], 16 * (EC // LAYERS))
                pool.dma_start(layer_rows[g][:].bitcast(I32),
                               layers[g][0:N * N, :].rearrange("(m p n) o -> p m (n o)", p=P, n=N)) \
                    .then_inc(layers_landed, 16)

            pool.wait_ge(norm_ready, NT - 1)
            pool.wait_ge(norm_last_ready, 1)
            pool.wait_ge(bo_landed, 16)
            for m in range(NT):
                pool.tensor_tensor(rows[:, m, :], rows[:, m, :], bo_all[:], ALU.add).then_inc(residual_ready, 1)

            def add_picked(j):
                pool.wait_ge(picked_ready, j + 1)
                if j:
                    pool.wait_ge(picked_used, j)
                pool.tensor_tensor(mask[:], mask[:], picked[j % 2][:], ALU.add).then_inc(picked_used, 1)

            ffn_integers(1)
            load_ffn(2)
            add_picked(0)
            add_picked(1)
            ffn_integers(2)
            load_ffn(3)
            add_picked(2)
            add_picked(3)
            pool.wait_ge(picked_used, 4)
            pool.sem_inc(mask_ready, 1)
            ffn_integers(3)
            load_ffn(4)
            ffn_integers(4)

            for h in range(HEADS):
                for m in range(NT):
                    pool.wait_ge(inv_ready, NT * h + m + 1)
                    pool.tensor_scalar(probs[h % 2][:, m, :], probs[h % 2][:, m, :], row_inv[:, h % 2, m:m + 1], 1.0,
                                       ALU.mult, ALU.mult).then_inc(probs_ready, 1)
                if h in WO_TAILS:
                    u = WO_TAILS.index(h)
                    pool.wait_ge(lo_split, unit(6, 0, AHEAD + u))
                    tail(6, 0, u)

            pool.wait_ge(scored, NT * HEADS)
            for t in range(KT):
                pool.tensor_scalar(diagonals[:, t * P:(t + 1) * P], ident[:], down_scale[:, t:t + 1], 1.0,
                                   ALU.mult, ALU.mult).then_inc(diagonals_ready, 1)

            for n in range(2 * NT):
                at = piece(n)
                pool.wait_ge(x_clipped, n + 1)
                pool.tensor_scalar(xqT[at], turned[at], -ROUND, 1.0, ALU.add, ALU.mult).then_inc(xq_ready, 1)

            for m in range(NT):
                pool.wait_ge(ffn_out_ready, m + 1)
                pool.tensor_tensor(rows[:, m, 0:HALF], rows[:, m, 0:HALF], ffn_out[:, m, 0:HALF], ALU.add) \
                    .then_inc(out_first, 1)

        @block.tensor
        def _(pe):
            def three(out_ap, a_hi, a_lo, b_hi, b_lo, first, last):
                pe.matmul(out_ap, a_hi, b_hi, start=first, stop=False)
                pe.matmul(out_ap, a_hi, b_lo, start=False, stop=False)
                return pe.matmul(out_ap, a_lo, b_hi, start=False, stop=last)

            pe.sem_inc(unit_done, RING)
            pe.sem_inc(y_ready, RING)

            pe.wait_ge(ident_ready, 1)
            for n in range(2 * NT):
                m, c = n // 2, n % 2
                if m < NT - 1:
                    pe.wait_ge(norm_ready, m + 1)
                else:
                    pe.wait_ge(norm_last_ready, 1)
                for j in range(4):
                    k = 4 * c + j
                    mm = pe.transpose(bank[2 + n][:, j * P:(j + 1) * P], normed[:, m, k * P:(k + 1) * P], ident[:])
                mm.then_inc(norm_turned, 1)

            def project(p):
                src_hi, src_lo = (xT_hi, xT_lo) if p % 2 == 0 else (yT_hi, yT_lo)
                if p == 0:
                    pe.wait_ge(xT_ready, 2 * NT)
                with pe.Fori(0, GROUPS) as g:
                    for r in range(RING):
                        u = unit(p, g, r)
                        pe.wait_ge(lo_split, u + 1)
                        pe.wait_ge(y_ready, u + 1)
                        for k in range(KT):
                            if p % 2 and r == 0 and k > KT - RING:
                                pe.wait_ge(y_ready, (p - 1) * KT + k + 1 + RING)
                            s = slice(k * P, (k + 1) * P)
                            mm = three(bank[r][:, 0:N], w_hi[r][:, s], w_lo[r][:, s], src_hi[:, k, :], src_lo[:, k, :],
                                       k == 0, k == KT - 1)
                        mm.then_inc(unit_done, 1)

            def turn_ffn(j):
                kind, t = FFN_JOBS[j]
                pe.wait_ge(ffn_rounded, j + 1)
                if j:
                    pe.wait_ge(ffn_ready, 2 * j)
                if kind == "gate_up":
                    for g, b in enumerate((4, 7)):
                        into = bank[b][:].bitcast(BF16)
                        for k in range(KT):
                            mm = pe.transpose(into[:, k * P:(k + 1) * P],
                                              ffn_int[:, g * F + k * P:g * F + (k + 1) * P], ident_b[:])
                else:
                    for it in range(IT):
                        into = bank[4 if it < 2 else 7][:].bitcast(BF16)
                        w = min(P, I - it * P)
                        for q in range(4):
                            c = (4 * (it % 2) + q) * P
                            mm = pe.transpose(into[0:w, c:c + P], ffn_int[:, q * I + it * P:q * I + it * P + w],
                                              ident_b[:])
                mm.then_inc(ffn_turned, 1)

            def scores(h):
                a, c = slice(h % 2 * D, (h % 2 + 1) * D), h // 2
                for m in range(NT):
                    if h:
                        pe.wait_ge(scored, NT * (h - 1) + m + 1)
                    else:
                        pe.wait_ge(v2_ready, m + 1)
                    n = slice(m * P, (m + 1) * P)
                    three(bank[m][:, 0:N], q2_hi[a, c, n], q2_lo[a, c, n], k2_hi[a, c, :], k2_lo[a, c, :],
                          True, True).then_inc(scores_done, 1)

            project(0)

            pe.wait_ge(compared, 2 * KT + 1)
            pe.matmul(bank[4][0:SPAN, 0:EC], overridden[0:EC, :], ident_b[0:EC, 0:EC], start=True, stop=True)
            pe.matmul(bank[4][64:64 + SPAN, 0:EC], overridden[64:64 + EC, :], ident_b[64:64 + EC, 64:64 + EC],
                      start=True, stop=True).then_inc(dead_ready, 1)

            project(1)
            turn_ffn(0)
            project(2)
            project(3)
            turn_ffn(1)
            project(4)
            turn_ffn(2)

            for h in range(2):
                for r in range(RING):
                    pe.wait_ge(lo_split, unit(5, h, r) + 1)
                    for b in range(2):
                        k = 2 * r + b
                        if h == 0:
                            pe.wait_ge(y_ready, 4 * KT + k + 1 + RING)
                        s = slice(b * HALF, (b + 1) * HALF)
                        for m in range(NT):
                            if h == 0 and k == 0:
                                pe.wait_ge(y_ready, 4 * KT + RING + m + 1 + RING)
                            n = slice(m * P, (m + 1) * P)
                            mm = three(bank[V2_BANKS[h][m]][:], yT_hi[:, k, n], yT_lo[:, k, n],
                                       w_hi[r][:, s], w_lo[r][:, s], k == 0, k == KT - 1)
                            if k == KT - 1 and m < NT - 1:
                                mm.then_inc(v2_done, 1)
                    mm.then_inc(unit_done, 1)
                turn_ffn(3 + h)
                if h == 0:
                    scores(0)

            def turn_probs(h):
                if h:
                    pe.wait_ge(pT_ready, NT * h)
                else:
                    pe.wait_ge(v2_ready, 2 * NT)
                    pe.wait_ge(ffn_ready, 10)
                for m in range(NT):
                    pe.wait_ge(probs_ready, NT * h + m + 1)
                    for c in range(NT):
                        mm = pe.transpose(bank[3 + c][:, m * P:(m + 1) * P], probs[h % 2][:, m, c * P:(c + 1) * P],
                                          ident[:])
                mm.then_inc(probs_turned, 1)

            def values(h):
                first = h // 2 * 2 * D
                width = D * (1 + h % 2)
                if h >= 2:
                    pe.wait_ge(o_ready, h - 1)
                for c in range(NT):
                    pe.wait_ge(pT_ready, NT * h + c + 1)
                    mm = three(bank[6 + h % 2][0:width, 0:N], v2_hi[:, c, first:first + width],
                               v2_lo[:, c, first:first + width], pT_hi[:, c, :], pT_lo[:, c, :], c == 0, c == NT - 1)
                mm.then_inc(values_done, 1)

            def output_unit(r):
                pe.wait_ge(lo_split, unit(6, 0, r) + 1)
                for b in range(2):
                    k = 2 * r + b
                    pe.wait_ge(o_ready, 2 * k + 2)
                    s = slice(b * HALF, (b + 1) * HALF)
                    for m in range(NT):
                        n = slice(m * P, (m + 1) * P)
                        mm = three(bank[m][:], yT_hi[:, k, n], yT_lo[:, k, n], w_hi[r][:, s], w_lo[r][:, s],
                                   k == 0, k == KT - 1)
                        if k == KT - 1 and m < NT - 1:
                            mm.then_inc(wo_done, 1)
                mm.then_inc(unit_done, 1)

            for i in range(1, HEADS):
                scores(i)
                if i >= 2:
                    values(i - 2)
                turn_probs(i - 1)
            values(HEADS - 2)
            pe.wait_ge(scored, NT * HEADS)
            output_unit(0)
            turn_probs(HEADS - 1)
            output_unit(1)
            values(HEADS - 1)
            output_unit(2)
            output_unit(3)
            pe.wait_ge(o_ready, HEADS)
            pe.wait_ge(diagonals_ready, KT)
            for t in range(KT):
                mm = pe.matmul(bank[6 + t // 4][:, t % 4 * P:(t % 4 + 1) * P], ones[:], diagonals[:, t * P:(t + 1) * P],
                               start=True, stop=True)
            mm.then_inc(spread_done, 1)
            pe.wait_ge(pT_ready, NT * HEADS)
            for m in range(NT):
                n = slice(m * P, (m + 1) * P)
                for k in range(KT):
                    if m == 0 and k % 2 == 0:
                        pe.wait_ge(lo_split, unit(6, 1, k // 2) + 1)
                    s = slice(k % 2 * HALF, (k % 2 + 1) * HALF)
                    mm = three(bank[3 + m][:], yT_hi[:, k, n], yT_lo[:, k, n], w_hi[k // 2][:, s], w_lo[k // 2][:, s],
                               k == 0, k == KT - 1)
                mm.then_inc(wo_done, 1)

            def top_as_row(n):
                pe.wait_ge(top_ready, n + 1)
                pe.transpose(bank[7][0:1, 0:P], top[:, n:n + 1], ident[:]).then_inc(top_row, 1)

            def spread_top(n):
                pe.wait_ge(top_one, n + 1)
                pe.matmul(bank[6][:, n:n + 1], ones[0:1, :], top[0:1, 2 + n:3 + n], start=True, stop=True) \
                    .then_inc(top_all, 1)

            pe.wait_ge(spread_ready, 2)
            for n in TURN_ORDER:
                c, m = n // NT, n % NT
                if n == 2:
                    top_as_row(0)
                pe.wait_ge(norm2_ready, m + 1)
                for j in range(4):
                    k = 4 * c + j
                    mm = pe.transpose(bank[n][:, j * P:(j + 1) * P], normed2[:, m, k * P:(k + 1) * P], ident[:])
                mm.then_inc(norm2_turned, 1)
                if n == 2:
                    spread_top(0)

            for g in range(2):
                for t in range(IT):
                    for k in range(KT):
                        if g == 0 and t == 0 and k % 4 == 0:
                            pe.wait_ge(xq_ready, 2 * NT if k else NT)
                        mm = pe.matmul(bank[GATE_UP_BANKS[g][t]][:, 0:N], gate_upT[:, k, g, t * P:(t + 1) * P],
                                       xqT[:, k, :], start=(k == 0), stop=(k == KT - 1))
                    mm.then_inc(gate_up_done, 1)
            top_as_row(1)
            spread_top(1)

            for m in range(NT):
                for h in range(2):
                    for t in range(IT):
                        if m == 0 and h == 0:
                            pe.wait_ge(hq_ready, t + 1)
                        w = min(P, I - t * P)
                        mm = pe.matmul(bank[2 * m + h][:], hqT[0:w, t, m * P:(m + 1) * P],
                                       downT[0:w, t, h * HALF:(h + 1) * HALF], start=(t == 0), stop=(t == IT - 1))
                    mm.then_inc(down_done, 1)

        @block.scalar
        def _(act):
            def head(p, g, r):
                n = (r + AHEAD) % RING
                groups = g + (p * GROUPS + (r + AHEAD) // RING)
                act.wait_ge(w_landed[n], groups * 16 + 16)
                act.wait_ge(unit_done, unit(p, g, r) + (AHEAD + 1))
                act.activation(w_hi[n][:], raw[n][:], ACT.Copy).then_inc(hi_split, 1)

            def head_of_first(u):
                act.wait_ge(w_landed[u], 16)
                act.activation(w_hi[u][:], raw[u][:], ACT.Copy).then_inc(hi_split, 1)

            def root(n, m):
                act.wait_ge(var_ready, NT * n + m + 1)
                act.activation(newton[:, 1, m:m + 1], newton[:, 2, m:m + 1], ACT.Sqrt).then_inc(root_ready, 1)

            def normalise(m):
                act.wait_ge(std_ready, m + 1)
                act.activation(normed[:, m, :], rows[:, m, :], ACT.Identity, bias=newton[:, 5, m:m + 1],
                               scale=newton[:, 0, m:m + 1]).then_inc(norm_ready, 1)

            root(0, 0)
            normalise(0)
            root(0, 1)
            head_of_first(0)
            root(0, 2)
            normalise(1)

            for n in range(2 * NT):
                m, c = n // 2, n % 2
                act.wait_ge(norm_turned, n + 1)
                act.activation(xT_hi[:, 4 * c:4 * c + 4, m * P:(m + 1) * P],
                               bank[2 + n][:].rearrange("p (k n) -> p k n", k=4), ACT.Copy).then_inc(xT_hi_ready, 1)

            head_of_first(1)
            act.wait_ge(blank_ready, NT + 1)
            for g in range(LAYERS):
                act.dma_start(layers[g][0:N * N, :].rearrange("(m p n) o -> p m (n o)", p=P, n=N),
                              (picked[0] if g else mask)[:].bitcast(I32)).then_inc(layers_cleared, 16)

            act.wait_ge(consts_landed, 48)
            act.activation(clip[:, 1, :], clip[:, 0, :], ACT.Exp, scale=-1.0).then_inc(softplus_exp, 1)
            act.activation(type_w[:, 1, :], type_w[:, 0, :], ACT.Abs).then_inc(act_step, 1)
            act.wait_ge(act_step, 1)
            act.activation(type_w[:, 2, :], type_w[:, 1, :], ACT.Exp, scale=-1.0).then_inc(act_step, 1)
            act.wait_ge(act_step, 2)
            act.activation(type_w[:, 3, :], type_w[:, 2, :], ACT.Ln, bias=1.0).then_inc(softplus_exp, 1)

            def project(p):
                dst = (yT_hi, q2_hi, yT_hi, k2_hi, yT_hi)[p]
                with act.Fori(0, GROUPS) as g:
                    for r in range(RING):
                        head(p, g, r)
                        act.wait_ge(unit_done, unit(p, g, r) + (1 + RING))
                        act.activation(dst[:, bass.ds(g * RING + r, 1), :].rearrange("p a n -> p (a n)"),
                                       bank[r][:, 0:N], ACT.Identity,
                                       bias=bias[:, p, bass.ds(g * RING + r, 1)]).then_inc(y_hi_ready, 1)

            def take_ffn(j):
                kind, t = FFN_JOBS[j]
                act.wait_ge(ffn_turned, j + 1)
                into = bank[4][:].bitcast(BF16)
                if kind == "gate_up":
                    ins = act.activation(gate_upT[:, :, 0, t * P:(t + 1) * P], into.rearrange("p (k i) -> p k i", k=KT),
                                         ACT.Copy)
                else:
                    ins = act.activation(downT[:, 0:2, 4 * t * P:4 * (t + 1) * P],
                                         into.rearrange("p (t f) -> p t f", t=2), ACT.Copy)
                ins.then_inc(ffn_ready, 1)

            def exponentials(h, tiles):
                b = h % 2
                for m in tiles:
                    act.wait_ge(scored, NT * h + m + 1)
                    act.activation(probs[b][:, m, :], probs[b][:, m, :], ACT.Exp, bias=neg_max[:, b, m:m + 1],
                                   scale=-1.0, accum_out=row_sum[:, b, m:m + 1]).then_inc(exp_ready, 1)

            project(0)
            project(1)
            take_ffn(0)
            project(2)
            project(3)
            take_ffn(1)
            project(4)
            take_ffn(2)

            for h in range(2):
                for r in range(RING):
                    head(5, h, r)
                for m in range(NT):
                    if m < NT - 1:
                        act.wait_ge(v2_done, 2 * h + m + 1)
                    else:
                        act.wait_ge(unit_done, unit(5, h, RING - 1) + 1 + RING)
                    act.activation(v2_hi[:, m, h * HALF:(h + 1) * HALF], bank[V2_BANKS[h][m]][:], ACT.Copy) \
                        .then_inc(v2_hi_ready, 1)
                if h == 0:
                    act.wait_ge(mask_ready, 1)
                take_ffn(3 + h)
                if h == 0:
                    exponentials(0, range(NT))

            def probs_head(h):
                act.wait_ge(probs_turned, h + 1)
                for c in range(NT):
                    act.activation(pT_hi[:, c, :], bank[3 + c][:, 0:N], ACT.Copy).then_inc(pT_hi_ready, 1)

            def output_head(h):
                a = slice(h % 2 * D, (h % 2 + 1) * D)
                act.wait_ge(values_done, h + 1)
                act.activation(yT_hi[a, h // 2, :], bank[6 + h % 2][a, 0:N], ACT.Identity,
                               bias=bias[a, 5, h // 2:h // 2 + 1]).then_inc(o_hi_ready, 1)

            for i in range(1, HEADS + 2):
                if i < HEADS:
                    exponentials(i, range(NT - 1))
                if i <= HEADS:
                    probs_head(i - 1)
                if i in WO_TAILS:
                    head(6, 0, WO_TAILS.index(i))
                if i < HEADS:
                    exponentials(i, (NT - 1,))
                if i >= 2:
                    output_head(i - 2)

            for r in range(2, RING + AHEAD):
                head(6, r // RING, r % RING)

            act.wait_ge(spread_done, 1)
            for b in range(2):
                act.activation(spread[:, b * HALF:(b + 1) * HALF], bank[6 + b][:], ACT.Copy).then_inc(spread_ready, 1)
            for m in range(NT):
                root(1, m)
            act.activation(clip[:, 1, :], clip[:, 0, :], ACT.Sigmoid).then_inc(softplus_exp, 1)

            act.wait_ge(quant_ready, 1)
            for n in range(2 * NT):
                act.wait_ge(norm2_turned, TURN_ORDER.index(n) + 1)
                act.activation(turned[piece(n)],
                               bank[n][:].rearrange("p (k n) -> p k n", k=4), ACT.Identity, bias=top[:, 8:9],
                               scale=top[:, 6:7]).then_inc(x_rounded, 1)

            for t in range(IT):
                act.wait_ge(gate_up_done, t + 1)
                act.activation(gate_s[:, t, :], bank[GATE_UP_BANKS[0][t]][:, 0:N], ACT.Sigmoid,
                               scale=act_scale[:, 0, t:t + 1]).then_inc(gate_sigmoid, 1)

        @block.vector
        def _(dve):
            steps = [0]

            def step(ins):
                ins.then_inc(dve_step, 1)
                steps[0] += 1
                dve.wait_ge(dve_step, steps[0])

            def f32(ap):
                return ap.bitcast(F32)

            def tail(p, g, r):
                n = (r + AHEAD) % RING
                dve.wait_ge(hi_split, unit(p, g, r) + (AHEAD + 1))
                dve.tensor_tensor(w_lo[n][:], raw[n][:], f32(w_hi[n][:]), ALU.subtract).then_inc(lo_split, 1)

            def variance(n, m):
                step(dve.bn_aggr(mean_var[:, m, :], stats[:, m, :, :]))
                dve.tensor_scalar(newton[:, 2, m:m + 1], mean_var[:, m, 1:2], EPS, None, ALU.add).then_inc(var_ready, 1)

            def inverse_std(n, m):
                y, root, v, t, u = (newton[:, i, m:m + 1] for i in range(5))
                dve.wait_ge(root_ready, NT * n + m + 1)
                step(dve.reciprocal(y, root))
                step(dve.scalar_tensor_tensor(out=t, in0=y, scalar=-0.5, in1=y, op0=ALU.mult, op1=ALU.mult))
                step(dve.tensor_tensor(u, t, v, ALU.mult))
                step(dve.scalar_tensor_tensor(out=y, in0=u, scalar=1.5, in1=y, op0=ALU.add, op1=ALU.mult))

            def normalise_last():
                m = NT - 1
                dve.tensor_scalar(normed[:, m, :], rows[:, m, :], mean_var[:, m, 0:1], newton[:, 0, m:m + 1],
                                  ALU.subtract, ALU.mult).then_inc(norm_last_ready, 1)

            def shift(m):
                dve.scalar_tensor_tensor(out=newton[:, 5, m:m + 1], in0=mean_var[:, m, 0:1], scalar=-1.0,
                                         in1=newton[:, 0, m:m + 1], op0=ALU.mult, op1=ALU.mult).then_inc(std_ready, 1)

            for m in range(NT + 1):
                if m < NT:
                    dve.wait_ge(x_landed[m], 16)
                    dve.bn_stats(stats[:, m, 0, :], rows[:, m, 0:HALF])
                    step(dve.bn_stats(stats[:, m, 1, :], rows[:, m, HALF:F]))
                    variance(0, m)
                if m:
                    inverse_std(0, m - 1)
                    if m < NT:
                        shift(m - 1)
                    else:
                        normalise_last()
            for n in range(2 * NT):
                m, c = n // 2, n % 2
                dve.wait_ge(xT_hi_ready, n + 1)
                at = (slice(0, P), slice(4 * c, 4 * c + 4), slice(m * P, (m + 1) * P))
                dve.tensor_tensor(xT_lo[at], bank[2 + n][:].rearrange("p (k n) -> p k n", k=4), f32(xT_hi[at]),
                                  ALU.subtract).then_inc(xT_ready, 1)

            dve.wait_ge(edges_landed, 16 * 5)
            dve.wait_ge(edge_consts, 1)
            step(dve.scalar_tensor_tensor(out=keys[:], in0=key_parts[:, 0, :], scalar=float(N), in1=key_parts[:, 1, :],
                                          op0=ALU.mult, op1=ALU.add))
            dve.sem_inc(compared, 1)
            step(dve.tensor_copy(edge_f[:], edge_i[:]))
            dve.tensor_scalar(edge_value[:, 0, :], edge_f[:, 2, :], 0.0, 4.0, ALU.is_equal, ALU.mult)
            dve.tensor_scalar(edge_value[:, 1, :], edge_f[:, 2, :], 4.0, -1.0, ALU.min, ALU.add)
            step(dve.scalar_tensor_tensor(out=edge_cell[:], in0=edge_f[:, 0, :], scalar=float(N), in1=edge_f[:, 1, :],
                                          op0=ALU.mult, op1=ALU.add))
            dve.tensor_scalar(edge_cell[:], edge_cell[:], spare_cell[:], None, ALU.subtract)
            step(dve.tensor_tensor(edge_value[:, 0, :], edge_value[:, 0, :], edge_value[:, 1, :], ALU.add))
            dve.tensor_tensor(cell_value[:, 1, :].bitcast(F32), edge_value[:, 0, :], edge_value[:, 2, :], ALU.add)

            def project(p):
                dst_lo = (yT_lo, q2_lo, yT_lo, k2_lo, yT_lo)[p]
                dst_hi = (yT_hi, q2_hi, yT_hi, k2_hi, yT_hi)[p]
                with dve.Fori(0, GROUPS) as g:
                    for r in range(RING):
                        if p == 0:
                            find_doubles(g, r)
                        else:
                            tail(p, g, r)
                        u = unit(p, g, r)
                        dve.wait_ge(y_hi_ready, u + 1)
                        c = bass.ds(g * RING + r, 1)
                        dve.scalar_tensor_tensor(out=dst_lo[:, c, :].rearrange("p a n -> p (a n)"), in0=bank[r][:, 0:N],
                                                 scalar=bias[:, p, c], in1=f32(dst_hi[:, c, :].rearrange("p a n -> p (a n)")),
                                                 op0=ALU.add, op1=ALU.subtract).then_inc(y_ready, 1)

            def find_doubles(g, r):
                w = SPAN // KT
                at = g * (RING * w) + r * w
                n = g * (2 * RING) + 2 * r
                own = keys[:, bass.ds(at, w)].unsqueeze(2).to_broadcast([P, w, P - 1])
                later = bass.AP(keys, at + 1, [[keys.shape[1], P], [1, w], [1, P - 1]])
                dve.wait_ge(compared, n + 1)
                dve.tensor_tensor(same[:], own, later, ALU.is_equal).then_inc(compared, 1)
                dve.wait_ge(compared, n + 2)
                dve.tensor_reduce(overridden[:, bass.ds(at, w)], same[:], AX.X, ALU.max).then_inc(compared, 1)

            def masked_max(h):
                b = h % 2
                for m in range(NT):
                    dve.wait_ge(scores_done, NT * h + m + 1)
                    if h >= 2:
                        dve.wait_ge(probs_turned, h - 1)
                    dve.tensor_tensor_reduce(out=probs[b][:, m, :], in0=bank[m][:, 0:N], in1=mask[:, m, :],
                                             scale=-SCALE, scalar=3.0e38, op0=ALU.add, op1=ALU.min,
                                             accum_out=neg_max[:, b, m:m + 1]).then_inc(scored, 1)

            def inverse_sums(h, tiles):
                b = h % 2
                for m in tiles:
                    dve.wait_ge(exp_ready, NT * h + m + 1)
                    dve.reciprocal(row_inv[:, b, m:m + 1], row_sum[:, b, m:m + 1]).then_inc(inv_ready, 1)

            def pick(j):
                if j >= 2:
                    dve.wait_ge(picked_used, j - 1)
                dve.tensor_scalar(picked[j % 2][:], classes[:], 2.0 ** 23 + j, type_w[:, 4, j:j + 1],
                                  ALU.is_equal, ALU.mult).then_inc(picked_ready, 1)

            def ffn_scales(j):
                kind, t = FFN_JOBS[j]
                dve.wait_ge(ffn_landed, 32 * (j + 1))
                if kind == "gate_up":
                    view, scale = ffn_raw[:].rearrange("p (t f) -> p t f", t=2), gate_up_scale[:, t, :]
                else:
                    view = ffn_raw[:, 0:4 * I].rearrange("p (t i) -> p t i", t=4)
                    scale = down_scale[:, 4 * t:4 * t + 4]
                n = view.shape[1]
                step(dve.tensor_reduce(scale, view, AX.X, ALU.max, apply_absolute_value=True))
                step(dve.tensor_scalar(scale, scale, 1e-30, 1.0 / QMAX, ALU.max, ALU.mult))
                dve.reciprocal(q_inv[:, 0:n], scale).then_inc(ffn_scaled, 1)

            def take_ffn(j):
                kind, t = FFN_JOBS[j]
                dve.wait_ge(ffn_turned, j + 1)
                into = bank[7][:].bitcast(BF16)
                if kind == "gate_up":
                    ins = dve.tensor_copy(gate_upT[:, :, 1, t * P:(t + 1) * P], into.rearrange("p (k i) -> p k i", k=KT))
                else:
                    w = I - 2 * P
                    ins = dve.tensor_copy(downT[0:w, 2, 4 * t * P:4 * (t + 1) * P], into[0:w, 0:4 * P])
                ins.then_inc(ffn_ready, 1)

            project(0)
            dve.wait_ge(dead_ready, 1)
            step(dve.tensor_scalar(alive[:], bank[4][:, 0:EC], -1.0, 1.0, ALU.mult, ALU.add))
            step(dve.tensor_tensor(edge_cell[:], edge_cell[:], alive[:], ALU.mult))
            dve.tensor_scalar(cell_value[:, 0, :], edge_cell[:], spare_cell[:], None, ALU.add).then_inc(cells_ready, 1)
            ffn_scales(0)
            dve.wait_ge(softplus_exp, 2)
            step(dve.tensor_scalar(type_w[:, 4, :], type_w[:, 0, :], 0.0, None, ALU.max))
            step(dve.tensor_tensor(type_w[:, 4, :], type_w[:, 4, :], type_w[:, 3, :], ALU.add))
            step(dve.tensor_scalar(type_w[:, 4, :], type_w[:, 4, :], 1.0 / SCALE, None, ALU.mult))
            step(dve.tensor_scalar(clip[:, 2, :], clip[:, 1, :], 1.0, None, ALU.add))
            step(dve.reciprocal(clip[:, 3, :], clip[:, 2, :]))
            step(dve.memset(top[:, 8:9], ROUND))
            dve.wait_ge(lo_split, KT + AHEAD)
            project(1)
            take_ffn(0)
            project(2)
            ffn_scales(1)
            project(3)
            take_ffn(1)
            ffn_scales(2)

            dve.wait_ge(layers_landed, 16 * LAYERS)
            dve.tensor_tensor(picked[0][:], picked[0][:], picked[1][:], ALU.max)
            step(dve.tensor_tensor(classes[:], classes[:], mask[:], ALU.max))
            step(dve.tensor_tensor(classes[:], classes[:], picked[0][:], ALU.max))
            step(dve.tensor_scalar(mask[:], classes[:], 0.0, NO_EDGE, ALU.is_equal, ALU.mult))
            step(dve.tensor_scalar(classes[:], classes[:], 2.0 ** 23, None, ALU.add))
            bits = classes[:].bitcast(I32)
            step(dve.tensor_scalar(bits, bits, 3, 0x4B000000, ALU.bitwise_and, ALU.bitwise_or))
            pick(0)
            pick(1)
            project(4)
            pick(2)
            pick(3)
            take_ffn(2)
            ffn_scales(3)

            for h in range(2):
                for r in range(RING):
                    tail(5, h, r)
                for m in range(NT):
                    s = slice(h * HALF, (h + 1) * HALF)
                    dve.wait_ge(v2_hi_ready, NT * h + m + 1)
                    dve.tensor_tensor(v2_lo[:, m, s], bank[V2_BANKS[h][m]][:], f32(v2_hi[:, m, s]), ALU.subtract) \
                        .then_inc(v2_ready, 1)
                if h == 0:
                    dve.wait_ge(mask_ready, 1)
                take_ffn(3 + h)
                if h == 0:
                    ffn_scales(4)
                    masked_max(0)
                    inverse_sums(0, range(NT))

            def probs_tail(h):
                for c in range(NT):
                    dve.wait_ge(pT_hi_ready, NT * h + c + 1)
                    dve.tensor_tensor(pT_lo[:, c, :], bank[3 + c][:, 0:N], f32(pT_hi[:, c, :]), ALU.subtract) \
                        .then_inc(pT_ready, 1)

            def output_tail(h):
                a = slice(h % 2 * D, (h % 2 + 1) * D)
                dve.wait_ge(o_hi_ready, h + 1)
                dve.scalar_tensor_tensor(out=yT_lo[a, h // 2, :], in0=bank[6 + h % 2][a, 0:N],
                                         scalar=bias[a, 5, h // 2:h // 2 + 1], in1=f32(yT_hi[a, h // 2, :]),
                                         op0=ALU.add, op1=ALU.subtract).then_inc(o_ready, 1)

            for i in range(1, HEADS + 3):
                if i < HEADS:
                    masked_max(i)
                if i >= 3:
                    output_tail(i - 3)
                if i < HEADS:
                    inverse_sums(i, range(NT - 1))
                if i <= HEADS:
                    probs_tail(i - 1)
                if i < HEADS:
                    inverse_sums(i, (NT - 1,))

            dve.wait_ge(lo_split, unit(6, 0, AHEAD + len(WO_TAILS)))
            for r in range(len(WO_TAILS), RING + AHEAD):
                tail(6, r // RING, r % RING)

            def normalise(m):
                dve.tensor_scalar(normed2[:, m, :], rows[:, m, :], mean_var[:, m, 0:1], newton[:, 0, m:m + 1],
                                  ALU.subtract, ALU.mult).then_inc(norm2_ready, 1)

            for h in range(2):
                for m in range(NT):
                    s = slice(h * HALF, (h + 1) * HALF)
                    if h == 0 and m == NT - 1:
                        dve.wait_ge(unit_done, unit(6, 0, RING - 1) + 1 + RING)
                    else:
                        dve.wait_ge(wo_done, (NT - 1) * h + m + 1)
                    dve.wait_ge(residual_ready, NT)
                    step(dve.tensor_tensor_reduce(out=rows[:, m, s], in0=bank[3 * h + m][:], in1=rows[:, m, s], scale=1.0,
                                                  scalar=-3.0e38, op0=ALU.add, op1=ALU.max,
                                                  accum_out=extremes[:, m, h, 0:1]))
                    dve.tensor_reduce(extremes[:, m, h, 1:2], rows[:, m, s], AX.X, ALU.min)
                    step(dve.bn_stats(stats[:, m, h, :], rows[:, m, s]))
                    if h == 1:
                        variance(1, m)
                        inverse_std(1, m)
                        ends = extremes[:, m, :, :].rearrange("p h e -> p (h e)")
                        step(dve.tensor_scalar(ends, ends, mean_var[:, m, 0:1], newton[:, 0, m:m + 1], ALU.subtract,
                                               ALU.mult))
                        if m < NT - 1:
                            normalise(m)
            dve.tensor_reduce(top[:, 0:1], extremes[:].rearrange("p m h e -> p (m h e)"), AX.X, ALU.max,
                              apply_absolute_value=True).then_inc(top_ready, 1)

            def top_of_row(n):
                dve.wait_ge(top_row, n + 1)
                dve.tensor_reduce(top[0:1, 2 + n:3 + n], bank[7][0:1, 0:P], AX.X, ALU.max).then_inc(top_one, 1)

            def scale_from_top(n):
                dve.wait_ge(top_all, n + 1)
                step(dve.tensor_scalar(top[:, 4 + n:5 + n], bank[6][:, n:n + 1], clip[:, 3, n:n + 1], 1.0 / QMAX,
                                       ALU.mult, ALU.mult))
                dve.reciprocal(top[:, 6 + n:7 + n], top[:, 4 + n:5 + n]).then_inc(quant_ready, 1)
                dve.wait_ge(quant_ready, n + 1)

            def clip_rounded(ap):
                return dve.tensor_scalar(ap, ap, ROUND + QMAX, ROUND - QMAX - 1.0, ALU.min, ALU.max)

            normalise(NT - 1)
            top_of_row(0)
            scale_from_top(0)
            for g in range(2):
                ins = dve.tensor_scalar(act_scale[:, g, :], gate_up_scale[:, :, g], top[:, 4:5], 1.0,
                                        ALU.mult, ALU.mult)
            step(ins)
            for n in range(2 * NT):
                dve.wait_ge(x_rounded, n + 1)
                clip_rounded(turned[piece(n)]).then_inc(x_clipped, 1)

            for t in range(IT):
                gate = gate_s[:, t, :]
                dve.wait_ge(gate_sigmoid, t + 1)
                ins = dve.scalar_tensor_tensor(out=gate, in0=bank[GATE_UP_BANKS[0][t]][:, 0:N],
                                               scalar=act_scale[:, 0, t:t + 1], in1=gate, op0=ALU.mult, op1=ALU.mult)
            step(ins)
            for t in range(IT):
                dve.wait_ge(gate_up_done, IT + t + 1)
                step(dve.scalar_tensor_tensor(out=hidden[:, t, :], in0=bank[GATE_UP_BANKS[1][t]][:, 0:N],
                                              scalar=act_scale[:, 1, t:t + 1], in1=gate_s[:, t, :],
                                              op0=ALU.mult, op1=ALU.mult))
                step(dve.tensor_reduce(top[:, 10 + t:11 + t], hidden[:, t, :], AX.X, ALU.max,
                                       apply_absolute_value=True))
            dve.tensor_reduce(top[:, 1:2], top[:, 10:10 + IT], AX.X, ALU.max).then_inc(top_ready, 1)
            top_of_row(1)
            scale_from_top(1)
            for t in range(IT):
                step(dve.tensor_scalar(hidden[:, t, :], hidden[:, t, :], top[:, 7:8], top[:, 8:9], ALU.mult, ALU.add))
                step(clip_rounded(hidden[:, t, :]))
                dve.tensor_scalar(hqT[:, t, :], hidden[:, t, :], -ROUND, None, ALU.add).then_inc(hq_ready, 1)

            for m in range(NT):
                for h in range(2):
                    s = slice(h * HALF, (h + 1) * HALF)
                    dve.wait_ge(down_done, 2 * m + h + 1)
                    ins = dve.scalar_tensor_tensor(out=ffn_out[:, m, s], in0=bank[2 * m + h][:], scalar=top[:, 5:6],
                                                   in1=spread[:, s], op0=ALU.mult, op1=ALU.mult)
                    if h == 0:
                        ins.then_inc(ffn_out_ready, 1)
                    else:
                        step(ins)
                        dve.tensor_tensor(rows[:, m, s], rows[:, m, s], ffn_out[:, m, s], ALU.add) \
                            .then_inc(out_second, 1)


def kernel(x, src, dst, edge_type_5, L0_gnn_edge_type_weights, L0_gnn_wq, L0_gnn_bq, L0_gnn_wk, L0_gnn_bk, L0_gnn_wv,
           L0_gnn_bv, L0_gnn_wiq, L0_gnn_biq, L0_gnn_wik, L0_gnn_bik, L0_gnn_wiv, L0_gnn_biv, L0_gnn_wo, L0_gnn_bo,
           L0_ffn_clip_x, L0_ffn_clip_down, L0_ffn_w_gate, L0_ffn_w_up, L0_ffn_w_down):
    import numpy as np
    import concourse.bacc as bacc
    from concourse.bass_utils import run_bass_kernel_spmd

    N, F = x.shape
    KT = F // P
    EC = src.shape[0] // P

    def block_units(w):
        return np.asarray(w).reshape(KT, P, KT, P).transpose(0, 3, 2, 1).reshape(KT, P, F)

    def half_units(w):
        return np.asarray(w).reshape(2, F // 2, KT // 2, 2, P).transpose(0, 2, 4, 3, 1).reshape(KT, P, F)

    def row_tiles(w):
        w = np.asarray(w)
        tiles = -(-w.shape[0] // P)
        return np.pad(w, ((0, tiles * P - w.shape[0]), (0, 0))).reshape(tiles, P, w.shape[1])

    weights = np.concatenate([block_units(w) for w in (L0_gnn_wq, L0_gnn_wiq, L0_gnn_wk, L0_gnn_wik, L0_gnn_wv)]
                             + [half_units(w) for w in (L0_gnn_wiv, L0_gnn_wo)])
    biases = (L0_gnn_bq, L0_gnn_biq, L0_gnn_bk, L0_gnn_bik, L0_gnn_bv, L0_gnn_biv)
    edges = [np.asarray(e).reshape(EC, P) for e in (src, dst, edge_type_5)]
    gate, up = row_tiles(L0_ffn_w_gate), row_tiles(L0_ffn_w_up)
    arrays = {
        "x_rows": np.asarray(x),
        "weights": weights,
        "bias_cols": np.stack([np.asarray(b).reshape(KT, P).T for b in biases], 1),
        "bo": np.asarray(L0_gnn_bo),
        "edge_cols": np.stack([e.T for e in edges]),
        "edge_rows": np.stack(edges[:2]),
        "type_weights": np.asarray(L0_gnn_edge_type_weights),
        "clips": np.concatenate([np.asarray(L0_ffn_clip_x), np.asarray(L0_ffn_clip_down)]),
        "w_gate_up": np.stack([gate, up], 1).reshape(2 * gate.shape[0], P, F),
        "w_down": row_tiles(L0_ffn_w_down),
    }
    arrays = {name: np.ascontiguousarray(a) for name, a in arrays.items()}
    nc = bacc.Bacc("TRN2", target_bir_lowering=False, num_devices=1)
    args = [nc.dram_tensor(name, a.shape, mybir.dt.from_np(a.dtype), kind="ExternalInput").ap()
            for name, a in arrays.items()]
    out = nc.dram_tensor("out_rows", (N, F), F32, kind="ExternalOutput").ap()
    layers = [nc.dram_tensor(f"layer{g}", (N * N + P, 1), mybir.dt.int32, kind="Internal").ap() for g in range(LAYERS)]
    gnn_ffn(nc, *args, layers, out)
    result = run_bass_kernel_spmd(nc, [arrays], core_ids=[0])
    return result.results[0]["out_rows"]
```

```python
from contextlib import ExitStack

import concourse.bass as bass
from concourse import mybir

P = 128
ALU = mybir.AluOpType
ACT = mybir.ActivationFunctionType
AX = mybir.AxisListType
F32 = mybir.dt.float32
F32R = mybir.dt.float32r
BF16 = mybir.dt.bfloat16
I32 = mybir.dt.int32

RING = 4
AHEAD = 2
LAYERS = 4
ROUND = 1.5 * 2.0 ** 23
QMAX = 127.0
NO_EDGE = -1.0e30
EPS = 1e-5
HEADS = 16
FFN_JOBS = [("gate_up", 0), ("gate_up", 1), ("gate_up", 2), ("down", 0), ("down", 1)]


def gnn_ffn(nc, x, weights, bias_cols, bo, edge_cols, edge_rows, type_weights, clips, w_gate_up, w_down, layers, out):
    N, F = x.shape
    NT = N // P
    KT = F // P
    HALF = F // 2
    D = F // HEADS
    EC = edge_cols.shape[2]
    SPAN = P // 2
    IT = w_gate_up.shape[0] // 2
    I = w_down.shape[2]
    SCALE = float(D) ** -0.5
    UNITS = weights.shape[0]
    GROUPS = KT // RING
    assert NT == 3 and KT == 8 and D == 64 and UNITS == 7 * KT and IT * P <= N
    assert EC % (2 * LAYERS) == 0 and EC <= 64 and 4 * (EC + 1) < 2 ** 20

    with ExitStack() as ctx:
        def sb(name, shape, dt, stack=ctx):
            return stack.enter_context(nc.sbuf_tensor(name, shape, dt))

        def sem(name):
            return ctx.enter_context(nc.semaphore(name))

        bank = [ctx.enter_context(nc.psum_tensor(f"bank{b}", [P, 512], F32)) for b in range(8)]

        rows = sb("rows", [P, NT, F], F32)
        raw = [sb(f"raw{r}", [P, F], F32) for r in range(RING)]
        w_hi = sb("w_hi", [P, RING, F], F32R)
        w_lo = sb("w_lo", [P, RING, F], F32R)
        mask = sb("mask", [P, NT, N], F32)
        gate_upT = sb("gate_upT", [P, KT, 2, IT * P], BF16)
        with ExitStack() as early:
            classes = sb("classes", [P, NT, N], F32, early)
        downT = sb("downT", [P, IT, F], BF16)
        ident = sb("ident", [P, P], F32)
        ident_b = sb("ident_b", [P, P], BF16)
        ones = sb("ones", [P, P], F32)
        bias = sb("bias", [P, 6, KT], F32)
        stats = sb("stats", [P, NT, 2, 6], F32)
        mean_var = sb("mean_var", [P, NT, 2], F32)
        newton = sb("newton", [P, 6, NT], F32)
        neg_max = sb("neg_max", [P, 2, NT], F32)
        row_sum = sb("row_sum", [P, 2, NT], F32)
        row_inv = sb("row_inv", [P, 2, NT], F32)
        type_w = sb("type_w", [P, 5, 4], F32)
        clip = sb("clip", [P, 4, 2], F32)
        gate_up_scale = sb("gate_up_scale", [P, IT, 2], F32)
        down_scale = sb("down_scale", [P, KT], F32)
        q_inv = sb("q_inv", [P, 4], F32)
        extremes = sb("extremes", [P, NT, 2, 2], F32)
        top = sb("top", [P, 24], F32)
        act_scale = sb("act_scale", [P, 2, IT], F32)
        k2_twice = [sb(f"k2_twice{b}", [P, N], F32R) for b in range(2)]
        cell_value = sb("cell_value", [P, 2, EC], I32)
        staged = [sb(f"staged{b}", [P, 2, LAYERS], I32) for b in range(2)]

        with ExitStack() as early:
            key_parts = sb("key_parts", [P, 2, 192], I32, early)
            keys = sb("keys", [P, 192], F32, early)
            same = sb("same", [P, SPAN // KT, P - 1], BF16, early)
            overridden = sb("overridden", [P, SPAN], BF16, early)
            bo_all = sb("bo_all", [P, F], F32, early)
            edge_i = sb("edge_i", [P, 3, EC], I32, early)
            edge_f = sb("edge_f", [P, 3, EC], F32, early)
            edge_value = sb("edge_value", [P, 3, EC], F32, early)
            edge_cell = sb("edge_cell", [P, EC], F32, early)
            alive = sb("alive", [P, EC], F32, early)
            spare_cell = sb("spare_cell", [P, 1], F32, early)
        with ExitStack() as late:
            turned = sb("turned", [P, KT, N], F32, late)
            xqT = sb("xqT", [P, KT, N], BF16, late)
            gate_s = sb("gate_s", [P, IT, N], F32, late)
            hidden = sb("hidden", [P, IT, N], F32, late)
            hqT = sb("hqT", [P, IT, N], BF16, late)
            diagonals = sb("diagonals", [P, F], F32, late)
            spread = sb("spread", [P, F], F32, late)
        k2_hi = sb("k2_hi", [P, KT, N], F32R)
        k2_lo = sb("k2_lo", [P, KT, N], F32R)
        q2 = [sb(f"q2_{b}", [P, KT, N], F32R) for b in range(2)]

        with ExitStack() as late:
            normed2 = sb("normed2", [P, NT, F], F32, late)
            ffn_out = sb("ffn_out", [P, NT, F], F32, late)
        xT_hi = sb("xT_hi", [P, KT, N], F32R)
        xT_lo = sb("xT_lo", [P, KT, N], F32R)
        v2_hi = xT_hi[:].rearrange("p a b -> p (a b)").rearrange("p (m f) -> p m f", m=NT)
        v2_lo = xT_lo[:].rearrange("p a b -> p (a b)").rearrange("p (m f) -> p m f", m=NT)

        with ExitStack() as early:
            normed = sb("normed", [P, NT, F], F32, early)
        yT_hi = sb("yT_hi", [P, KT, N], F32R)
        yT_lo = sb("yT_lo", [P, KT, N], F32R)

        with ExitStack() as early:
            picked = [sb(f"picked{b}", [P, NT, N], F32, early) for b in range(2)]
            ffn_raw = sb("ffn_raw", [P, 2 * F], F32, early)
            ffn_int = sb("ffn_int", [P, 2 * F], BF16, early)
        probs = [sb(f"probs{b}", [P, NT, N], F32) for b in range(2)]
        pT_hi, pT_lo = ([sb(name, [P, NT, N], F32R)[:],
                         w[:, 2:RING, :].rearrange("p r f -> p (r f)")[:, 0:NT * N].rearrange("p (c n) -> p c n", c=NT)]
                        for name, w in (("pT_hi", w_hi), ("pT_lo", w_lo)))

        x_landed = [sem(f"x_landed{n}") for n in range(2 * NT)]
        consts_landed = sem("consts_landed")
        edges_landed = sem("edges_landed")
        bo_landed = sem("bo_landed")
        w_landed = [sem(f"w_landed{r}") for r in range(RING)]
        ffn_first_landed = sem("ffn_first_landed")
        ffn_landed = sem("ffn_landed")
        ident_ready = sem("ident_ready")
        dve_step = sem("dve_step")
        act_step = sem("act_step")
        pool_step = sem("pool_step")
        compared = sem("compared")
        dead_ready = sem("dead_ready")
        blank_ready = sem("blank_ready")
        edge_consts = sem("edge_consts")
        layers_cleared = sem("layers_cleared")
        cells_ready = sem("cells_ready")
        edges_staged = sem("edges_staged")
        chunk_turn = sem("chunk_turn")
        written = [sem(f"written{g}") for g in range(LAYERS)]
        layers_landed = sem("layers_landed")
        picked_ready = sem("picked_ready")
        picked_used = sem("picked_used")
        keys_cleared = sem("keys_cleared")
        softplus_exp = sem("softplus_exp")
        mask_ready = sem("mask_ready")
        var_ready = sem("var_ready")
        root_ready = sem("root_ready")
        std_ready = sem("std_ready")
        norm_ready = sem("norm_ready")
        norm_last_ready = sem("norm_last_ready")
        norm_turned = sem("norm_turned")
        xT_hi_ready = sem("xT_hi_ready")
        xT_ready = sem("xT_ready")
        hi_split = sem("hi_split")
        lo_split = sem("lo_split")
        unit_done = sem("unit_done")
        y_hi_ready = sem("y_hi_ready")
        y_ready = sem("y_ready")
        ffn_scaled = sem("ffn_scaled")
        ffn_rounded = sem("ffn_rounded")
        ffn_turned = sem("ffn_turned")
        ffn_ready = sem("ffn_ready")
        v2_done = sem("v2_done")
        v2_hi_ready = sem("v2_hi_ready")
        v2_ready = sem("v2_ready")
        k2_doubled = [sem(f"k2_doubled{b}") for b in range(2)]
        scores_done = sem("scores_done")
        scored = sem("scored")
        exp_ready = sem("exp_ready")
        inv_ready = sem("inv_ready")
        probs_ready = sem("probs_ready")
        probs_turned = sem("probs_turned")
        pT_hi_ready = sem("pT_hi_ready")
        pT_ready = sem("pT_ready")
        values_done = sem("values_done")
        o_hi_ready = sem("o_hi_ready")
        o_ready = sem("o_ready")
        residual_ready = sem("residual_ready")
        wo_done = sem("wo_done")
        norm2_ready = sem("norm2_ready")
        norm2_turned = sem("norm2_turned")
        top_ready = sem("top_ready")
        top_row = sem("top_row")
        top_one = sem("top_one")
        top_all = sem("top_all")
        quant_ready = sem("quant_ready")
        x_rounded = sem("x_rounded")
        x_clipped = sem("x_clipped")
        xq_ready = sem("xq_ready")
        xq_last_ready = sem("xq_last_ready")
        gate_up_done = sem("gate_up_done")
        gate_sigmoid = sem("gate_sigmoid")
        hq_ready = sem("hq_ready")
        down_done = sem("down_done")
        diagonals_ready = sem("diagonals_ready")
        spread_done = sem("spread_done")
        spread_ready = sem("spread_ready")
        ffn_out_ready = sem("ffn_out_ready")
        out_first = sem("out_first")
        out_second = sem("out_second")
        stored = sem("stored")

        layer_rows = (mask, classes, picked[0], picked[1])
        GATE_UP_BANKS = ((0, 1, 2), (3, 4, 5))
        TURN_ORDER = (0, 1, 3, 4, 2, 5)
        ACT_PIECES = (0, 2, 3, 5)
        ACT_LAST = (4, 5)
        DVE_ORDER = (1, 0, 2, 4, 3, 5)
        HALVES = (slice(0, D), slice(D, 2 * D))
        V2_BANKS = ((0, 1, 2), (5, 6, 3))

        def double_k2(queue, h):
            for to in HALVES:
                queue.dma_start(k2_twice[h % 2][to, :].bitcast(F32), k2_hi[HALVES[h % 2], h // 2, :].bitcast(F32)) \
                    .then_inc(k2_doubled[h % 2], 16)

        def piece(n):
            c, m = n // NT, n % NT
            return slice(0, P), slice(4 * c, 4 * c + 4), slice(m * P, (m + 1) * P)

        def unit(p, g, r):
            return g * RING + (p * KT + r)

        block = ctx.enter_context(nc.Block())

        @block.sync
        def _(sp):
            for m in range(NT):
                for h in range(2):
                    s = slice(h * HALF, (h + 1) * HALF)
                    sp.dma_start(rows[:, m, s], x.rearrange("(m p) f -> p m f", p=P)[:, m, s]) \
                        .then_inc(x_landed[2 * m + h], 16)
            for r in range(RING):
                sp.dma_start(raw[r][:], weights[r]).then_inc(w_landed[r], 16)
            sp.dma_start(edge_i[:], edge_cols.rearrange("a p c -> p a c")).then_inc(edges_landed, 16)
            sp.wait_ge(keys_cleared, 1)
            for a in range(2):
                sp.dma_start(key_parts[0:EC, a, 0:P], edge_rows[a]).then_inc(edges_landed, 16)
                sp.dma_start(key_parts[64:64 + EC, a, 0:SPAN], edge_rows[a][:, SPAN:P]).then_inc(edges_landed, 16)
            for g in range(2):
                sp.dma_start(ffn_raw[:, g * F:(g + 1) * F], w_gate_up[g]).then_inc(ffn_first_landed, 16)
            sp.dma_start(bo_all[:], bo.partition_broadcast(P)).then_inc(bo_landed, 16)

            def load_group(g):
                for r in range(RING):
                    sp.wait_ge(hi_split, g * RING + (r + 1 - RING))
                    sp.wait_ge(lo_split, g * RING + (r + 1 - RING))
                    sp.dma_start(raw[r][:], weights[bass.ds(g * RING + r, 1)].rearrange("a p f -> (a p) f")) \
                        .then_inc(w_landed[r], 16)

            with sp.Fori(1, UNITS // RING - 1) as g:
                load_group(g)
            for h in range(3, HEADS):
                sp.wait_ge(scores_done, NT * (h - 1))
                double_k2(sp, h)
            load_group(UNITS // RING - 1)
            def store(m, first, last):
                sp.dma_start(out.rearrange("(m p) f -> p m f", p=P)[:, m, first:last], rows[:, m, first:last]) \
                    .then_inc(stored, 16)

            for m in range(NT):
                sp.wait_ge(out_first, m + 1)
                store(m, 0, HALF)
                if m < NT - 1:
                    sp.wait_ge(out_second, m + 1)
                    store(m, HALF, F)
            for q in range(2):
                sp.wait_ge(out_second, NT + q)
                store(NT - 1, HALF + q * HALF // 2, HALF + (q + 1) * HALF // 2)
            sp.wait_ge(stored, 16 * (2 * NT + 1))

        @block.gpsimd
        def _(pool):
            steps = [0]

            def step(ins):
                ins.then_inc(pool_step, 1)
                steps[0] += 1
                pool.wait_ge(pool_step, steps[0])

            step(pool.memset(ones[:], 1.0))
            step(pool.affine_select(out=ident[:], in_=ones[:], compare_op=ALU.is_equal, fill=0.0, base=0,
                                    pattern=[[-1, P]], channel_multiplier=1))
            pool.tensor_copy(ident_b[:], ident[:]).then_inc(ident_ready, 1)
            pool.memset(key_parts[:], -1).then_inc(keys_cleared, 1)
            pool.dma_start(type_w[:, 0, :], type_weights.partition_broadcast(P)).then_inc(consts_landed, 16)
            pool.dma_start(clip[:, 0, :], clips.partition_broadcast(P)).then_inc(consts_landed, 16)
            pool.dma_start(bias[:], bias_cols).then_inc(consts_landed, 16)
            pool.memset(picked[0][:], 0.0).then_inc(blank_ready, 1)
            step(pool.memset(mask[:], 0.0))
            pool.wait_ge(ident_ready, 1)
            for m in range(NT):
                pool.tensor_scalar(mask[:, m, m * P:(m + 1) * P], ident[:], 3.0, 1.0, ALU.mult, ALU.mult) \
                    .then_inc(blank_ready, 1)
            step(pool.iota(edge_value[:, 2, :], [[4, EC]], base=4, channel_multiplier=0,
                           allow_small_or_imprecise_dtypes=True))
            step(pool.iota(spare_cell[:], [[0, 1]], base=0, channel_multiplier=1, allow_small_or_imprecise_dtypes=True))
            pool.tensor_scalar(spare_cell[:], spare_cell[:], float(N * N), 1.0, ALU.add, ALU.mult).then_inc(edge_consts, 1)
            for u in range(AHEAD):
                pool.wait_ge(hi_split, u + 1)
                pool.tensor_tensor(w_lo[:, u, :], raw[u][:], w_hi[:, u, :].bitcast(F32), ALU.subtract).then_inc(lo_split, 1)
            def load_ffn(j):
                kind, t = FFN_JOBS[j]
                pool.wait_ge(ffn_rounded, j)
                if kind == "gate_up":
                    for g in range(2):
                        pool.dma_start(ffn_raw[:, g * F:(g + 1) * F], w_gate_up[2 * t + g]).then_inc(ffn_landed, 16)
                else:
                    for g in range(2):
                        pool.dma_start(ffn_raw[:, 2 * g * I:(2 * g + 2) * I].rearrange("p (t i) -> p t i", t=2),
                                       w_down[4 * t + 2 * g:4 * t + 2 * g + 2].rearrange("t p i -> p t i")) \
                            .then_inc(ffn_landed, 16)

            def ffn_integers(j):
                width, tiles = (F, 2) if FFN_JOBS[j][0] == "gate_up" else (I, 4)
                pool.wait_ge(ffn_scaled, j + 1)
                for g in range(tiles):
                    s = slice(g * width, (g + 1) * width)
                    step(pool.tensor_scalar(ffn_raw[:, s], ffn_raw[:, s], q_inv[:, g:g + 1], ROUND, ALU.mult, ALU.add))
                if j:
                    pool.wait_ge(ffn_turned, j)
                s = slice(0, tiles * width)
                pool.tensor_scalar(ffn_int[:, s], ffn_raw[:, s], -ROUND, 1.0, ALU.add, ALU.mult) \
                    .then_inc(ffn_rounded, 1)

            def tail(p, g, r):
                n = (r + AHEAD) % RING
                pool.wait_ge(hi_split, unit(p, g, r) + (AHEAD + 1))
                pool.tensor_tensor(w_lo[:, n, :], raw[n][:], w_hi[:, n, :].bitcast(F32), ALU.subtract).then_inc(lo_split, 1)

            with pool.Fori(0, GROUPS) as g:
                for r in range(RING):
                    tail(0, g, r)
            ffn_integers(0)
            load_ffn(1)

            pool.wait_ge(norm_ready, NT - 1)
            pool.wait_ge(norm_last_ready, 1)
            pool.wait_ge(bo_landed, 16)
            for m in range(NT):
                pool.tensor_tensor(rows[:, m, :], rows[:, m, :], bo_all[:], ALU.add).then_inc(residual_ready, 1)

            pool.wait_ge(cells_ready, 1)
            pool.wait_ge(layers_cleared, 16 * LAYERS)
            pool.sem_inc(edges_staged, 1)

            def write_chunks(i, first):
                for b in range(2):
                    pool.tensor_copy(staged[b][:], cell_value[:, :, bass.ds(i * (2 * LAYERS) + b * LAYERS, LAYERS)]) \
                        .then_inc(edges_staged, 1)
                    pool.wait_ge(edges_staged, i * 2 + b + 2)
                    for g in range(LAYERS):
                        if b or not first:
                            pool.wait_ge(written[g], (i * 2 + b) * 16)
                        pool.sem_inc(chunk_turn, 1)
                        pool.indirect_dma_start(layers[g], bass.IndirectOffsetOnAxis(ap=staged[b][:, 0, g:g + 1], axis=0),
                                                staged[b][:, 1, g:g + 1], None).then_inc(written[g], 16)

            write_chunks(0, True)
            with pool.Fori(1, EC // (2 * LAYERS)) as i:
                write_chunks(i, False)
            for g in range(LAYERS):
                pool.wait_ge(written[g], 16 * (EC // LAYERS))
                pool.dma_start(layer_rows[g][:].bitcast(I32),
                               layers[g][0:N * N, :].rearrange("(m p n) o -> p m (n o)", p=P, n=N)) \
                    .then_inc(layers_landed, 16)

            def add_picked(j):
                pool.wait_ge(picked_ready, j + 1)
                if j:
                    pool.wait_ge(picked_used, j)
                pool.tensor_tensor(mask[:], mask[:], picked[j % 2][:], ALU.add).then_inc(picked_used, 1)

            for j in range(1, 3):
                ffn_integers(j)
                load_ffn(j + 1)
            for j in range(4):
                add_picked(j)
            pool.wait_ge(picked_used, 4)
            pool.sem_inc(mask_ready, 1)
            ffn_integers(3)
            load_ffn(4)
            ffn_integers(4)

            for h in range(HEADS):
                for m in range(NT):
                    pool.wait_ge(inv_ready, NT * h + m + 1)
                    pool.tensor_scalar(probs[h % 2][:, m, :], probs[h % 2][:, m, :], row_inv[:, h % 2, m:m + 1], 1.0,
                                       ALU.mult, ALU.mult).then_inc(probs_ready, 1)

            pool.wait_ge(scored, NT * HEADS)
            for t in range(KT):
                pool.tensor_scalar(diagonals[:, t * P:(t + 1) * P], ident[:], down_scale[:, t:t + 1], 1.0,
                                   ALU.mult, ALU.mult).then_inc(diagonals_ready, 1)

            for n in DVE_ORDER:
                if n in ACT_LAST:
                    continue
                at = piece(n)
                pool.wait_ge(x_clipped, DVE_ORDER.index(n) + 1)
                pool.tensor_scalar(xqT[at], turned[at], -ROUND, 1.0, ALU.add, ALU.mult).then_inc(xq_ready, 1)

            for m in range(NT):
                pool.wait_ge(ffn_out_ready, m + 1)
                pool.tensor_tensor(rows[:, m, 0:HALF], rows[:, m, 0:HALF], ffn_out[:, m, 0:HALF], ALU.add) \
                    .then_inc(out_first, 1)

        @block.tensor
        def _(pe):
            def three(out_ap, a_hi, a_lo, b_hi, b_lo, first, last):
                pe.matmul(out_ap, a_hi, b_hi, start=first, stop=False)
                pe.matmul(out_ap, a_hi, b_lo, start=False, stop=False)
                return pe.matmul(out_ap, a_lo, b_hi, start=False, stop=last)

            pe.sem_inc(unit_done, RING)
            pe.sem_inc(y_ready, RING)

            pe.wait_ge(ident_ready, 1)
            for n in range(2 * NT):
                m, c = n // 2, n % 2
                if m < NT - 1:
                    pe.wait_ge(norm_ready, m + 1)
                else:
                    pe.wait_ge(norm_last_ready, 1)
                for j in range(4):
                    k = 4 * c + j
                    mm = pe.transpose(bank[2 + n][:, j * P:(j + 1) * P], normed[:, m, k * P:(k + 1) * P], ident[:])
                mm.then_inc(norm_turned, 1)

            def project(p):
                src_hi, src_lo = (xT_hi, xT_lo) if p % 2 == 0 else (yT_hi, yT_lo)
                with pe.Fori(0, GROUPS) as g:
                    for r in range(RING):
                        u = unit(p, g, r)
                        pe.wait_ge(lo_split, u + 1)
                        pe.wait_ge(y_ready, u + 1)
                        for k in range(KT):
                            if p == 0 and r == 0 and k % 4 == 0:
                                pe.wait_ge(xT_ready, 2 * NT if k else 2 * NT - 1)
                            if p % 2 and r == 0 and k > KT - RING:
                                pe.wait_ge(y_ready, (p - 1) * KT + k + 1 + RING)
                            s = slice(k * P, (k + 1) * P)
                            mm = three(bank[r][:, 0:N], w_hi[:, r, s], w_lo[:, r, s], src_hi[:, k, :], src_lo[:, k, :],
                                       k == 0, k == KT - 1)
                        mm.then_inc(unit_done, 1)

            def turn_ffn(j):
                kind, t = FFN_JOBS[j]
                pe.wait_ge(ffn_rounded, j + 1)
                if j:
                    pe.wait_ge(ffn_ready, 2 * j)
                if kind == "gate_up":
                    for g, b in enumerate((4, 7)):
                        into = bank[b][:].bitcast(BF16)
                        for k in range(KT):
                            mm = pe.transpose(into[:, k * P:(k + 1) * P],
                                              ffn_int[:, g * F + k * P:g * F + (k + 1) * P], ident_b[:])
                else:
                    for it in range(IT):
                        into = bank[4 if it < 2 else 7][:].bitcast(BF16)
                        w = min(P, I - it * P)
                        for q in range(4):
                            c = (4 * (it % 2) + q) * P
                            mm = pe.transpose(into[0:w, c:c + P], ffn_int[:, q * I + it * P:q * I + it * P + w],
                                              ident_b[:])
                mm.then_inc(ffn_turned, 1)

            def scores(h):
                a, c = HALVES[h % 2], h // 2
                pe.wait_ge(k2_doubled[h % 2], 32 * (h // 2 + 1))
                for m in range(NT):
                    if h:
                        pe.wait_ge(scored, NT * (h - 1) + m + 1)
                    else:
                        pe.wait_ge(v2_ready, m + 1)
                    n = slice(m * P, (m + 1) * P)
                    pe.matmul(bank[m][:, 0:N], q2[h % 2][:, c, n], k2_twice[h % 2][:], start=True, stop=False)
                    pe.matmul(bank[m][:, 0:N], q2[h % 2][a, c, n], k2_lo[a, c, :], start=False, stop=True) \
                        .then_inc(scores_done, 1)

            project(0)

            pe.wait_ge(compared, 2 * KT + 1)
            pe.matmul(bank[4][0:SPAN, 0:EC], overridden[0:EC, :], ident_b[0:EC, 0:EC], start=True, stop=True)
            pe.matmul(bank[4][64:64 + SPAN, 0:EC], overridden[64:64 + EC, :], ident_b[64:64 + EC, 64:64 + EC],
                      start=True, stop=True).then_inc(dead_ready, 1)

            project(1)
            turn_ffn(0)
            project(2)
            project(3)
            turn_ffn(1)
            project(4)
            turn_ffn(2)

            for h in range(2):
                for r in range(RING):
                    pe.wait_ge(lo_split, unit(5, h, r) + 1)
                    for b in range(2):
                        k = 2 * r + b
                        if h == 0:
                            pe.wait_ge(y_ready, 4 * KT + k + 1 + RING)
                        s = slice(b * HALF, (b + 1) * HALF)
                        for m in range(NT):
                            if h == 0 and k == 0:
                                pe.wait_ge(y_ready, 4 * KT + RING + m + 1 + RING)
                            n = slice(m * P, (m + 1) * P)
                            mm = three(bank[V2_BANKS[h][m]][:], yT_hi[:, k, n], yT_lo[:, k, n],
                                       w_hi[:, r, s], w_lo[:, r, s], k == 0, k == KT - 1)
                            if k == KT - 1 and m < NT - 1:
                                mm.then_inc(v2_done, 1)
                    mm.then_inc(unit_done, 1)
                    if h == 1 and r == 1:
                        scores(1)
                turn_ffn(3 + h)
                if h == 0:
                    scores(0)

            def turn_probs(h):
                if h:
                    pe.wait_ge(pT_ready, NT * h)
                else:
                    pe.wait_ge(v2_ready, 2 * NT)
                    pe.wait_ge(ffn_ready, 10)
                for m in range(NT):
                    pe.wait_ge(probs_ready, NT * h + m + 1)
                    for c in range(NT):
                        mm = pe.transpose(bank[3 + c][:, m * P:(m + 1) * P], probs[h % 2][:, m, c * P:(c + 1) * P],
                                          ident[:])
                mm.then_inc(probs_turned, 1)

            def values(h):
                first = h // 2 * 2 * D
                width = D * (1 + h % 2)
                if h >= 2:
                    pe.wait_ge(o_ready, h - 1)
                for c in range(NT):
                    pe.wait_ge(pT_ready, NT * h + c + 1)
                    mm = three(bank[6 + h % 2][0:width, 0:N], v2_hi[:, c, first:first + width],
                               v2_lo[:, c, first:first + width], pT_hi[h % 2][:, c, :], pT_lo[h % 2][:, c, :], c == 0, c == NT - 1)
                mm.then_inc(values_done, 1)

            def output_unit(r):
                pe.wait_ge(lo_split, unit(6, 0, r) + 1)
                for b in range(2):
                    k = 2 * r + b
                    pe.wait_ge(o_ready, 2 * k + 2)
                    s = slice(b * HALF, (b + 1) * HALF)
                    for m in range(NT):
                        n = slice(m * P, (m + 1) * P)
                        mm = three(bank[m][:], yT_hi[:, k, n], yT_lo[:, k, n], w_hi[:, r, s], w_lo[:, r, s],
                                   k == 0, k == KT - 1)
                        if k == KT - 1 and m < NT - 1:
                            mm.then_inc(wo_done, 1)
                mm.then_inc(unit_done, 1)

            for i in range(1, HEADS):
                if i > 1:
                    scores(i)
                turn_probs(i - 1)
                if i >= 2:
                    values(i - 2)
            values(HEADS - 2)
            turn_probs(HEADS - 1)
            pe.wait_ge(scored, NT * HEADS)
            output_unit(0)
            values(HEADS - 1)
            output_unit(1)
            output_unit(2)
            output_unit(3)
            pe.wait_ge(o_ready, HEADS)
            pe.wait_ge(diagonals_ready, KT)
            for t in range(KT):
                mm = pe.matmul(bank[6 + t // 4][:, t % 4 * P:(t % 4 + 1) * P], ones[:], diagonals[:, t * P:(t + 1) * P],
                               start=True, stop=True)
            mm.then_inc(spread_done, 1)
            pe.wait_ge(pT_ready, NT * HEADS)
            for m in range(NT):
                n = slice(m * P, (m + 1) * P)
                for k in range(KT):
                    if m == 0 and k % 2 == 0:
                        pe.wait_ge(lo_split, unit(6, 1, k // 2) + 1)
                    s = slice(k % 2 * HALF, (k % 2 + 1) * HALF)
                    mm = three(bank[3 + m][:], yT_hi[:, k, n], yT_lo[:, k, n], w_hi[:, k // 2, s], w_lo[:, k // 2, s],
                               k == 0, k == KT - 1)
                mm.then_inc(wo_done, 1)

            def keep_warm(count):
                for _ in range(count):
                    pe.matmul(bank[7][:, 0:IT * P], gate_upT[:, 0, 0, 0:P], gate_upT[:, 0, 0, :], start=True, stop=True)

            def top_as_row(n):
                pe.wait_ge(top_ready, n + 1)
                pe.transpose(bank[7][0:1, 0:P], top[:, n:n + 1], ident[:]).then_inc(top_row, 1)

            def spread_top(n):
                pe.wait_ge(top_one, n + 1)
                pe.matmul(bank[6][:, n:n + 1], ones[0:1, :], top[0:1, 2 + n:3 + n], start=True, stop=True) \
                    .then_inc(top_all, 1)

            pe.wait_ge(spread_ready, 2)
            for n in TURN_ORDER:
                c, m = n // NT, n % NT
                if n == 2:
                    keep_warm(10)
                    top_as_row(0)
                    spread_top(0)
                pe.wait_ge(norm2_ready, m + 1)
                for j in range(4):
                    k = 4 * c + j
                    mm = pe.transpose(bank[n][:, j * P:(j + 1) * P], normed2[:, m, k * P:(k + 1) * P], ident[:])
                mm.then_inc(norm2_turned, 1)
            keep_warm(12)

            def gate_up(g, t, blocks):
                for k in blocks:
                    mm = pe.matmul(bank[GATE_UP_BANKS[g][t]][:, 0:N], gate_upT[:, k, g, t * P:(t + 1) * P],
                                   xqT[:, k, :], start=(k == 0), stop=(k == KT - 1))
                if k == KT - 1:
                    mm.then_inc(gate_up_done, 1)

            pe.wait_ge(xq_ready, NT)
            for t in range(IT):
                gate_up(0, t, range(KT // 2))
            pe.wait_ge(xq_ready, 2 * NT - len(ACT_LAST))
            pe.wait_ge(xq_last_ready, len(ACT_LAST))
            for t in range(IT):
                gate_up(0, t, range(KT // 2, KT))
            for t in range(IT):
                gate_up(1, t, range(KT))
            keep_warm(8)
            top_as_row(1)
            spread_top(1)
            keep_warm(8)

            for m in range(NT):
                for h in range(2):
                    for t in range(IT):
                        if m == 0 and h == 0:
                            pe.wait_ge(hq_ready, t + 1)
                        w = min(P, I - t * P)
                        mm = pe.matmul(bank[2 * m + h][:], hqT[0:w, t, m * P:(m + 1) * P],
                                       downT[0:w, t, h * HALF:(h + 1) * HALF], start=(t == 0), stop=(t == IT - 1))
                    mm.then_inc(down_done, 1)

        @block.scalar
        def _(act):
            def head(p, g, r):
                n = (r + AHEAD) % RING
                groups = g + (p * GROUPS + (r + AHEAD) // RING)
                act.wait_ge(w_landed[n], groups * 16 + 16)
                act.wait_ge(unit_done, unit(p, g, r) + (AHEAD + 1))
                act.activation(w_hi[:, n, :], raw[n][:], ACT.Copy).then_inc(hi_split, 1)

            def head_of_first(u):
                act.wait_ge(w_landed[u], 16)
                act.activation(w_hi[:, u, :], raw[u][:], ACT.Copy).then_inc(hi_split, 1)

            def root(n, m):
                act.wait_ge(var_ready, NT * n + m + 1)
                act.activation(newton[:, 1, m:m + 1], newton[:, 2, m:m + 1], ACT.Sqrt).then_inc(root_ready, 1)

            def normalise(m):
                act.wait_ge(std_ready, m + 1)
                act.activation(normed[:, m, :], rows[:, m, :], ACT.Identity, bias=newton[:, 5, m:m + 1],
                               scale=newton[:, 0, m:m + 1]).then_inc(norm_ready, 1)

            root(0, 0)
            normalise(0)
            root(0, 1)
            head_of_first(0)
            root(0, 2)
            normalise(1)

            for n in range(2 * NT):
                m, c = n // 2, n % 2
                act.wait_ge(norm_turned, n + 1)
                act.activation(xT_hi[:, 4 * c:4 * c + 4, m * P:(m + 1) * P],
                               bank[2 + n][:].rearrange("p (k n) -> p k n", k=4), ACT.Copy).then_inc(xT_hi_ready, 1)

            head_of_first(1)
            act.wait_ge(blank_ready, NT + 1)
            for g in range(LAYERS):
                act.dma_start(layers[g][0:N * N, :].rearrange("(m p n) o -> p m (n o)", p=P, n=N),
                              (picked[0] if g else mask)[:].bitcast(I32)).then_inc(layers_cleared, 16)

            act.wait_ge(consts_landed, 48)
            act.activation(clip[:, 1, :], clip[:, 0, :], ACT.Exp, scale=-1.0).then_inc(softplus_exp, 1)
            act.activation(type_w[:, 1, :], type_w[:, 0, :], ACT.Abs).then_inc(act_step, 1)
            act.wait_ge(act_step, 1)
            act.activation(type_w[:, 2, :], type_w[:, 1, :], ACT.Exp, scale=-1.0).then_inc(act_step, 1)
            act.wait_ge(act_step, 2)
            act.activation(type_w[:, 3, :], type_w[:, 2, :], ACT.Ln, bias=1.0).then_inc(softplus_exp, 1)

            def project(p):
                with act.Fori(0, GROUPS) as g:
                    for r in range(RING):
                        head(p, g, r)
                        act.wait_ge(unit_done, unit(p, g, r) + (1 + RING))
                        c = bass.ds(g * RING + r, 1)

                        def result(dst, of):
                            return act.activation(dst[of, c, :].rearrange("p a n -> p (a n)"), bank[r][of, 0:N],
                                                  ACT.Identity, bias=bias[of, p, c])

                        if p == 1:
                            for half, of in enumerate(HALVES):
                                ins = result(q2[half], of)
                        else:
                            ins = result(k2_hi if p == 3 else yT_hi, slice(0, P))
                        ins.then_inc(y_hi_ready, 1)

            def take_ffn(j):
                kind, t = FFN_JOBS[j]
                act.wait_ge(ffn_turned, j + 1)
                into = bank[4][:].bitcast(BF16)
                if kind == "gate_up":
                    ins = act.activation(gate_upT[:, :, 0, t * P:(t + 1) * P], into.rearrange("p (k i) -> p k i", k=KT),
                                         ACT.Copy)
                else:
                    ins = act.activation(downT[:, 0:2, 4 * t * P:4 * (t + 1) * P],
                                         into.rearrange("p (t f) -> p t f", t=2), ACT.Copy)
                ins.then_inc(ffn_ready, 1)

            def exponentials(h, tiles):
                b = h % 2
                for m in tiles:
                    act.wait_ge(scored, NT * h + m + 1)
                    act.activation(probs[b][:, m, :], probs[b][:, m, :], ACT.Exp, bias=neg_max[:, b, m:m + 1],
                                   scale=-1.0, accum_out=row_sum[:, b, m:m + 1]).then_inc(exp_ready, 1)

            project(0)
            project(1)
            take_ffn(0)
            project(2)
            act.wait_ge(residual_ready, NT)
            project(3)
            act.wait_ge(y_hi_ready, 4 * KT)
            double_k2(act, 0)
            double_k2(act, 1)
            take_ffn(1)
            project(4)
            take_ffn(2)

            for h in range(2):
                for r in range(RING):
                    head(5, h, r)
                    if h == 1 and r == 1:
                        exponentials(1, range(NT))
                for m in range(NT):
                    if m < NT - 1:
                        act.wait_ge(v2_done, 2 * h + m + 1)
                    else:
                        act.wait_ge(unit_done, unit(5, h, RING - 1) + 1 + RING)
                    act.activation(v2_hi[:, m, h * HALF:(h + 1) * HALF], bank[V2_BANKS[h][m]][:], ACT.Copy) \
                        .then_inc(v2_hi_ready, 1)
                if h == 0:
                    act.wait_ge(mask_ready, 1)
                take_ffn(3 + h)
                if h == 0:
                    exponentials(0, range(NT))
                    act.wait_ge(scores_done, NT)
                    double_k2(act, 2)

            def probs_head(h):
                act.wait_ge(probs_turned, h + 1)
                for c in range(NT):
                    act.activation(pT_hi[h % 2][:, c, :], bank[3 + c][:, 0:N], ACT.Copy).then_inc(pT_hi_ready, 1)

            def output_head(h):
                a = slice(h % 2 * D, (h % 2 + 1) * D)
                act.wait_ge(values_done, h + 1)
                act.activation(yT_hi[a, h // 2, :], bank[6 + h % 2][a, 0:N], ACT.Identity,
                               bias=bias[a, 5, h // 2:h // 2 + 1]).then_inc(o_hi_ready, 1)

            for i in range(1, HEADS + 2):
                if 1 < i < HEADS:
                    exponentials(i, range(NT - 1))
                if i <= HEADS:
                    probs_head(i - 1)
                if 1 < i < HEADS:
                    exponentials(i, (NT - 1,))
                if i >= 2:
                    output_head(i - 2)

            for r in range(RING + AHEAD):
                head(6, r // RING, r % RING)

            act.wait_ge(spread_done, 1)
            for b in range(2):
                act.activation(spread[:, b * HALF:(b + 1) * HALF], bank[6 + b][:], ACT.Copy).then_inc(spread_ready, 1)
            for m in range(NT):
                root(1, m)
            act.activation(clip[:, 1, :], clip[:, 0, :], ACT.Sigmoid).then_inc(softplus_exp, 1)

            act.wait_ge(quant_ready, 1)
            for n in ACT_PIECES:
                act.wait_ge(norm2_turned, TURN_ORDER.index(n) + 1)
                act.activation(turned[piece(n)],
                               bank[n][:].rearrange("p (k n) -> p k n", k=4), ACT.Identity, bias=top[:, 8:9],
                               scale=top[:, 6:7]).then_inc(x_rounded, 1)

            for n in ACT_LAST:
                act.wait_ge(x_clipped, DVE_ORDER.index(n) + 1)
                act.activation(xqT[piece(n)], turned[piece(n)], ACT.Identity, bias=top[:, 9:10]).then_inc(xq_last_ready, 1)

            for t in range(IT):
                act.wait_ge(gate_up_done, t + 1)
                act.activation(gate_s[:, t, :], bank[GATE_UP_BANKS[0][t]][:, 0:N], ACT.Sigmoid,
                               scale=act_scale[:, 0, t:t + 1]).then_inc(gate_sigmoid, 1)

        @block.vector
        def _(dve):
            steps = [0]

            def step(ins):
                ins.then_inc(dve_step, 1)
                steps[0] += 1
                dve.wait_ge(dve_step, steps[0])

            def f32(ap):
                return ap.bitcast(F32)

            def tail(p, g, r):
                n = (r + AHEAD) % RING
                dve.wait_ge(hi_split, unit(p, g, r) + (AHEAD + 1))
                dve.tensor_tensor(w_lo[:, n, :], raw[n][:], f32(w_hi[:, n, :]), ALU.subtract).then_inc(lo_split, 1)

            def variance(n, m):
                step(dve.bn_aggr(mean_var[:, m, :], stats[:, m, :, :]))
                dve.tensor_scalar(newton[:, 2, m:m + 1], mean_var[:, m, 1:2], EPS, None, ALU.add).then_inc(var_ready, 1)

            def inverse_std(n, m):
                y, root, v, t, u = (newton[:, i, m:m + 1] for i in range(5))
                dve.wait_ge(root_ready, NT * n + m + 1)
                step(dve.reciprocal(y, root))
                step(dve.scalar_tensor_tensor(out=t, in0=y, scalar=-0.5, in1=y, op0=ALU.mult, op1=ALU.mult))
                step(dve.tensor_tensor(u, t, v, ALU.mult))
                step(dve.scalar_tensor_tensor(out=y, in0=u, scalar=1.5, in1=y, op0=ALU.add, op1=ALU.mult))

            def normalise_last():
                m = NT - 1
                dve.tensor_scalar(normed[:, m, :], rows[:, m, :], mean_var[:, m, 0:1], newton[:, 0, m:m + 1],
                                  ALU.subtract, ALU.mult).then_inc(norm_last_ready, 1)

            def shift(m):
                dve.scalar_tensor_tensor(out=newton[:, 5, m:m + 1], in0=mean_var[:, m, 0:1], scalar=-1.0,
                                         in1=newton[:, 0, m:m + 1], op0=ALU.mult, op1=ALU.mult).then_inc(std_ready, 1)

            for m in range(NT + 1):
                if m < NT:
                    dve.wait_ge(x_landed[2 * m], 16)
                    dve.bn_stats(stats[:, m, 0, :], rows[:, m, 0:HALF])
                    dve.wait_ge(x_landed[2 * m + 1], 16)
                    step(dve.bn_stats(stats[:, m, 1, :], rows[:, m, HALF:F]))
                    variance(0, m)
                if m:
                    inverse_std(0, m - 1)
                    if m < NT:
                        shift(m - 1)
                    else:
                        normalise_last()
            for n in range(2 * NT):
                m, c = n // 2, n % 2
                dve.wait_ge(xT_hi_ready, n + 1)
                at = (slice(0, P), slice(4 * c, 4 * c + 4), slice(m * P, (m + 1) * P))
                dve.tensor_tensor(xT_lo[at], bank[2 + n][:].rearrange("p (k n) -> p k n", k=4), f32(xT_hi[at]),
                                  ALU.subtract).then_inc(xT_ready, 1)

            dve.wait_ge(edges_landed, 16 * 5)
            dve.wait_ge(edge_consts, 1)
            step(dve.scalar_tensor_tensor(out=keys[:], in0=key_parts[:, 0, :], scalar=float(N), in1=key_parts[:, 1, :],
                                          op0=ALU.mult, op1=ALU.add))
            dve.sem_inc(compared, 1)
            step(dve.tensor_copy(edge_f[:], edge_i[:]))
            dve.tensor_scalar(edge_value[:, 0, :], edge_f[:, 2, :], 0.0, 4.0, ALU.is_equal, ALU.mult)
            dve.tensor_scalar(edge_value[:, 1, :], edge_f[:, 2, :], 4.0, -1.0, ALU.min, ALU.add)
            step(dve.scalar_tensor_tensor(out=edge_cell[:], in0=edge_f[:, 0, :], scalar=float(N), in1=edge_f[:, 1, :],
                                          op0=ALU.mult, op1=ALU.add))
            dve.tensor_scalar(edge_cell[:], edge_cell[:], spare_cell[:], None, ALU.subtract)
            step(dve.tensor_tensor(edge_value[:, 0, :], edge_value[:, 0, :], edge_value[:, 1, :], ALU.add))
            dve.tensor_tensor(cell_value[:, 1, :].bitcast(F32), edge_value[:, 0, :], edge_value[:, 2, :], ALU.add)

            def project(p, groups=None):
                if groups is None:
                    with dve.Fori(0, GROUPS) as g:
                        project_group(p, g)
                for g in groups or ():
                    project_group(p, g)

            def project_group(p, g):
                for r in range(RING):
                    if p == 0:
                        find_doubles(g, r)
                    else:
                        tail(p, g, r)
                    u = unit(p, g, r)
                    dve.wait_ge(y_hi_ready, u + 1)
                    c = bass.ds(g * RING + r, 1)

                    def result_tail(dst, to, heads, of):
                        return dve.scalar_tensor_tensor(out=dst[to, c, :].rearrange("p a n -> p (a n)"),
                                                        in0=bank[r][of, 0:N], scalar=bias[of, p, c],
                                                        in1=f32(heads[of, c, :].rearrange("p a n -> p (a n)")),
                                                        op0=ALU.add, op1=ALU.subtract)

                    if p == 1:
                        for half, of in enumerate(HALVES):
                            ins = result_tail(q2[half], HALVES[1 - half], q2[half], of)
                    elif p == 3:
                        ins = result_tail(k2_lo, slice(0, P), k2_hi, slice(0, P))
                    else:
                        ins = result_tail(yT_lo, slice(0, P), yT_hi, slice(0, P))
                    ins.then_inc(y_ready, 1)

            def find_doubles(g, r):
                w = SPAN // KT
                at = g * (RING * w) + r * w
                n = g * (2 * RING) + 2 * r
                own = keys[:, bass.ds(at, w)].unsqueeze(2).to_broadcast([P, w, P - 1])
                later = bass.AP(keys, at + 1, [[keys.shape[1], P], [1, w], [1, P - 1]])
                dve.wait_ge(compared, n + 1)
                dve.tensor_tensor(same[:], own, later, ALU.is_equal).then_inc(compared, 1)
                dve.wait_ge(compared, n + 2)
                dve.tensor_reduce(overridden[:, bass.ds(at, w)], same[:], AX.X, ALU.max).then_inc(compared, 1)

            def masked_max(h):
                b = h % 2
                for m in range(NT):
                    dve.wait_ge(scores_done, NT * h + m + 1)
                    if h >= 2:
                        dve.wait_ge(probs_turned, h - 1)
                    dve.tensor_tensor_reduce(out=probs[b][:, m, :], in0=bank[m][:, 0:N], in1=mask[:, m, :],
                                             scale=-SCALE, scalar=3.0e38, op0=ALU.add, op1=ALU.min,
                                             accum_out=neg_max[:, b, m:m + 1]).then_inc(scored, 1)

            def inverse_sums(h, first, last):
                b = h % 2
                dve.wait_ge(exp_ready, NT * h + last + 1)
                dve.reciprocal(row_inv[:, b, first:last + 1], row_sum[:, b, first:last + 1]) \
                    .then_inc(inv_ready, last + 1 - first)

            def pick(j):
                if j >= 2:
                    dve.wait_ge(picked_used, j - 1)
                dve.tensor_scalar(picked[j % 2][:], classes[:], 2.0 ** 23 + j, type_w[:, 4, j:j + 1],
                                  ALU.is_equal, ALU.mult).then_inc(picked_ready, 1)

            def ffn_scales(j):
                kind, t = FFN_JOBS[j]
                if j:
                    dve.wait_ge(ffn_landed, 32 * j)
                else:
                    dve.wait_ge(ffn_first_landed, 32)
                if kind == "gate_up":
                    view, scale = ffn_raw[:].rearrange("p (t f) -> p t f", t=2), gate_up_scale[:, t, :]
                else:
                    view = ffn_raw[:, 0:4 * I].rearrange("p (t i) -> p t i", t=4)
                    scale = down_scale[:, 4 * t:4 * t + 4]
                n = view.shape[1]
                step(dve.tensor_reduce(scale, view, AX.X, ALU.max, apply_absolute_value=True))
                step(dve.tensor_scalar(scale, scale, 1e-30, 1.0 / QMAX, ALU.max, ALU.mult))
                dve.reciprocal(q_inv[:, 0:n], scale).then_inc(ffn_scaled, 1)

            def take_ffn(j):
                kind, t = FFN_JOBS[j]
                dve.wait_ge(ffn_turned, j + 1)
                into = bank[7][:].bitcast(BF16)
                if kind == "gate_up":
                    ins = dve.tensor_copy(gate_upT[:, :, 1, t * P:(t + 1) * P], into.rearrange("p (k i) -> p k i", k=KT))
                else:
                    w = I - 2 * P
                    ins = dve.tensor_copy(downT[0:w, 2, 4 * t * P:4 * (t + 1) * P], into[0:w, 0:4 * P])
                ins.then_inc(ffn_ready, 1)

            ffn_scales(0)
            project(0)
            dve.wait_ge(dead_ready, 1)
            step(dve.tensor_scalar(alive[:], bank[4][:, 0:EC], -1.0, 1.0, ALU.mult, ALU.add))
            step(dve.tensor_tensor(edge_cell[:], edge_cell[:], alive[:], ALU.mult))
            dve.tensor_scalar(cell_value[:, 0, :], edge_cell[:], spare_cell[:], None, ALU.add).then_inc(cells_ready, 1)
            dve.wait_ge(softplus_exp, 2)
            step(dve.tensor_scalar(type_w[:, 4, :], type_w[:, 0, :], 0.0, None, ALU.max))
            step(dve.tensor_tensor(type_w[:, 4, :], type_w[:, 4, :], type_w[:, 3, :], ALU.add))
            step(dve.tensor_scalar(type_w[:, 4, :], type_w[:, 4, :], 1.0 / SCALE, None, ALU.mult))
            step(dve.tensor_scalar(clip[:, 2, :], clip[:, 1, :], 1.0, None, ALU.add))
            step(dve.reciprocal(clip[:, 3, :], clip[:, 2, :]))
            dve.memset(top[:, 8:9], ROUND)
            step(dve.memset(top[:, 9:10], -ROUND))
            dve.wait_ge(lo_split, KT + AHEAD)
            project(1)
            take_ffn(0)
            ffn_scales(1)
            project(2)

            dve.wait_ge(residual_ready, NT)
            project(3, range(GROUPS // 2))
            dve.wait_ge(layers_landed, 16 * LAYERS)
            dve.tensor_tensor(picked[0][:], picked[0][:], picked[1][:], ALU.max)
            step(dve.tensor_tensor(classes[:], classes[:], mask[:], ALU.max))
            step(dve.tensor_tensor(classes[:], classes[:], picked[0][:], ALU.max))
            step(dve.tensor_scalar(mask[:], classes[:], 0.0, NO_EDGE, ALU.is_equal, ALU.mult))
            project(3, range(GROUPS // 2, GROUPS))
            take_ffn(1)
            ffn_scales(2)
            project(4, range(GROUPS // 2))
            step(dve.tensor_scalar(classes[:], classes[:], 2.0 ** 23, None, ALU.add))
            bits = classes[:].bitcast(I32)
            step(dve.tensor_scalar(bits, bits, 3, 0x4B000000, ALU.bitwise_and, ALU.bitwise_or))
            pick(0)
            pick(1)
            project(4, range(GROUPS // 2, GROUPS))
            pick(2)
            pick(3)
            take_ffn(2)
            ffn_scales(3)

            for h in range(2):
                for r in range(RING):
                    tail(5, h, r)
                    if h == 1 and r == 1:
                        masked_max(1)
                        inverse_sums(1, 0, NT - 1)
                for m in range(NT):
                    s = slice(h * HALF, (h + 1) * HALF)
                    dve.wait_ge(v2_hi_ready, NT * h + m + 1)
                    dve.tensor_tensor(v2_lo[:, m, s], bank[V2_BANKS[h][m]][:], f32(v2_hi[:, m, s]), ALU.subtract) \
                        .then_inc(v2_ready, 1)
                if h == 0:
                    dve.wait_ge(mask_ready, 1)
                take_ffn(3 + h)
                if h == 0:
                    ffn_scales(4)
                    masked_max(0)
                    inverse_sums(0, 0, NT - 1)

            def probs_tail(h):
                for c in range(NT):
                    dve.wait_ge(pT_hi_ready, NT * h + c + 1)
                    dve.tensor_tensor(pT_lo[h % 2][:, c, :], bank[3 + c][:, 0:N], f32(pT_hi[h % 2][:, c, :]), ALU.subtract) \
                        .then_inc(pT_ready, 1)

            def output_tail(h):
                a = slice(h % 2 * D, (h % 2 + 1) * D)
                dve.wait_ge(o_hi_ready, h + 1)
                dve.scalar_tensor_tensor(out=yT_lo[a, h // 2, :], in0=bank[6 + h % 2][a, 0:N],
                                         scalar=bias[a, 5, h // 2:h // 2 + 1], in1=f32(yT_hi[a, h // 2, :]),
                                         op0=ALU.add, op1=ALU.subtract).then_inc(o_ready, 1)

            for i in range(1, HEADS + 3):
                if 1 < i < HEADS:
                    masked_max(i)
                if i >= 3:
                    output_tail(i - 3)
                if 1 < i < HEADS:
                    inverse_sums(i, 0, NT - 2)
                if i <= HEADS:
                    probs_tail(i - 1)
                if 1 < i < HEADS:
                    inverse_sums(i, NT - 1, NT - 1)

            for r in range(RING + AHEAD):
                tail(6, r // RING, r % RING)

            def normalise(m):
                dve.tensor_scalar(normed2[:, m, :], rows[:, m, :], mean_var[:, m, 0:1], newton[:, 0, m:m + 1],
                                  ALU.subtract, ALU.mult).then_inc(norm2_ready, 1)

            for h in range(2):
                for m in range(NT):
                    s = slice(h * HALF, (h + 1) * HALF)
                    if h == 0 and m == NT - 1:
                        dve.wait_ge(unit_done, unit(6, 0, RING - 1) + 1 + RING)
                    else:
                        dve.wait_ge(wo_done, (NT - 1) * h + m + 1)
                    dve.wait_ge(residual_ready, NT)
                    step(dve.tensor_tensor_reduce(out=rows[:, m, s], in0=bank[3 * h + m][:], in1=rows[:, m, s], scale=1.0,
                                                  scalar=-3.0e38, op0=ALU.add, op1=ALU.max,
                                                  accum_out=extremes[:, m, h, 0:1]))
                    step(dve.bn_stats(stats[:, m, h, :], rows[:, m, s]))
                    if h == 1:
                        variance(1, m)
                    dve.tensor_reduce(extremes[:, m, h, 1:2], rows[:, m, s], AX.X, ALU.min)
                    if h == 1:
                        inverse_std(1, m)
                        ends = extremes[:, m, :, :].rearrange("p h e -> p (h e)")
                        step(dve.tensor_scalar(ends, ends, mean_var[:, m, 0:1], newton[:, 0, m:m + 1], ALU.subtract,
                                               ALU.mult))
                        if m < NT - 1:
                            normalise(m)
            dve.tensor_reduce(top[:, 0:1], extremes[:].rearrange("p m h e -> p (m h e)"), AX.X, ALU.max,
                              apply_absolute_value=True).then_inc(top_ready, 1)

            def top_of_row(n):
                dve.wait_ge(top_row, n + 1)
                dve.tensor_reduce(top[0:1, 2 + n:3 + n], bank[7][0:1, 0:P], AX.X, ALU.max).then_inc(top_one, 1)

            def scale_from_top(n):
                dve.wait_ge(top_all, n + 1)
                step(dve.tensor_scalar(top[:, 4 + n:5 + n], bank[6][:, n:n + 1], clip[:, 3, n:n + 1], 1.0 / QMAX,
                                       ALU.mult, ALU.mult))
                dve.reciprocal(top[:, 6 + n:7 + n], top[:, 4 + n:5 + n]).then_inc(quant_ready, 1)
                dve.wait_ge(quant_ready, n + 1)

            def clip_rounded(ap):
                return dve.tensor_scalar(ap, ap, ROUND + QMAX, ROUND - QMAX - 1.0, ALU.min, ALU.max)

            top_of_row(0)
            normalise(NT - 1)
            scale_from_top(0)
            for g in range(2):
                ins = dve.tensor_scalar(act_scale[:, g, :], gate_up_scale[:, :, g], top[:, 4:5], 1.0,
                                        ALU.mult, ALU.mult)
            step(ins)
            for n in DVE_ORDER:
                if n in ACT_PIECES:
                    dve.wait_ge(x_rounded, ACT_PIECES.index(n) + 1)
                else:
                    dve.wait_ge(norm2_turned, TURN_ORDER.index(n) + 1)
                    step(dve.tensor_scalar(turned[piece(n)], bank[n][:].rearrange("p (k n) -> p k n", k=4), top[:, 6:7],
                                           top[:, 8:9], ALU.mult, ALU.add))
                clip_rounded(turned[piece(n)]).then_inc(x_clipped, 1)

            for t in range(IT):
                gate = gate_s[:, t, :]
                dve.wait_ge(gate_sigmoid, t + 1)
                ins = dve.scalar_tensor_tensor(out=gate, in0=bank[GATE_UP_BANKS[0][t]][:, 0:N],
                                               scalar=act_scale[:, 0, t:t + 1], in1=gate, op0=ALU.mult, op1=ALU.mult)
            step(ins)
            for t in range(IT):
                dve.wait_ge(gate_up_done, IT + t + 1)
                step(dve.scalar_tensor_tensor(out=hidden[:, t, :], in0=bank[GATE_UP_BANKS[1][t]][:, 0:N],
                                              scalar=act_scale[:, 1, t:t + 1], in1=gate_s[:, t, :],
                                              op0=ALU.mult, op1=ALU.mult))
                step(dve.tensor_reduce(top[:, 10 + t:11 + t], hidden[:, t, :], AX.X, ALU.max,
                                       apply_absolute_value=True))
            dve.tensor_reduce(top[:, 1:2], top[:, 10:10 + IT], AX.X, ALU.max).then_inc(top_ready, 1)
            top_of_row(1)
            scale_from_top(1)
            for t in range(IT):
                step(dve.tensor_scalar(hidden[:, t, :], hidden[:, t, :], top[:, 7:8], top[:, 8:9], ALU.mult, ALU.add))
                step(clip_rounded(hidden[:, t, :]))
                dve.tensor_scalar(hqT[:, t, :], hidden[:, t, :], -ROUND, None, ALU.add).then_inc(hq_ready, 1)

            for m in range(NT):
                for h in range(2):
                    s = slice(h * HALF, (h + 1) * HALF)
                    dve.wait_ge(down_done, 2 * m + h + 1)
                    ins = dve.scalar_tensor_tensor(out=ffn_out[:, m, s], in0=bank[2 * m + h][:], scalar=top[:, 5:6],
                                                   in1=spread[:, s], op0=ALU.mult, op1=ALU.mult)
                    if h == 0:
                        ins.then_inc(ffn_out_ready, 1)
                    else:
                        step(ins)
                        parts = 2 if m == NT - 1 else 1
                        for q in range(parts):
                            s = slice(HALF + q * HALF // parts, HALF + (q + 1) * HALF // parts)
                            dve.tensor_tensor(rows[:, m, s], rows[:, m, s], ffn_out[:, m, s], ALU.add) \
                                .then_inc(out_second, 1)


def kernel(x, src, dst, edge_type_5, L0_gnn_edge_type_weights, L0_gnn_wq, L0_gnn_bq, L0_gnn_wk, L0_gnn_bk, L0_gnn_wv,
           L0_gnn_bv, L0_gnn_wiq, L0_gnn_biq, L0_gnn_wik, L0_gnn_bik, L0_gnn_wiv, L0_gnn_biv, L0_gnn_wo, L0_gnn_bo,
           L0_ffn_clip_x, L0_ffn_clip_down, L0_ffn_w_gate, L0_ffn_w_up, L0_ffn_w_down):
    import numpy as np
    import concourse.bacc as bacc
    from concourse.bass_utils import run_bass_kernel_spmd

    N, F = x.shape
    KT = F // P
    EC = src.shape[0] // P

    def block_units(w):
        return np.asarray(w).reshape(KT, P, KT, P).transpose(0, 3, 2, 1).reshape(KT, P, F)

    def half_units(w):
        return np.asarray(w).reshape(2, F // 2, KT // 2, 2, P).transpose(0, 2, 4, 3, 1).reshape(KT, P, F)

    def row_tiles(w):
        w = np.asarray(w)
        tiles = -(-w.shape[0] // P)
        return np.pad(w, ((0, tiles * P - w.shape[0]), (0, 0))).reshape(tiles, P, w.shape[1])

    weights = np.concatenate([block_units(w) for w in (L0_gnn_wq, L0_gnn_wiq, L0_gnn_wk, L0_gnn_wik, L0_gnn_wv)]
                             + [half_units(w) for w in (L0_gnn_wiv, L0_gnn_wo)])
    biases = (L0_gnn_bq, L0_gnn_biq, L0_gnn_bk, L0_gnn_bik, L0_gnn_bv, L0_gnn_biv)
    edges = [np.asarray(e).reshape(EC, P) for e in (src, dst, edge_type_5)]
    gate, up = row_tiles(L0_ffn_w_gate), row_tiles(L0_ffn_w_up)
    arrays = {
        "x_rows": np.asarray(x),
        "weights": weights,
        "bias_cols": np.stack([np.asarray(b).reshape(KT, P).T for b in biases], 1),
        "bo": np.asarray(L0_gnn_bo),
        "edge_cols": np.stack([e.T for e in edges]),
        "edge_rows": np.stack(edges[:2]),
        "type_weights": np.asarray(L0_gnn_edge_type_weights),
        "clips": np.concatenate([np.asarray(L0_ffn_clip_x), np.asarray(L0_ffn_clip_down)]),
        "w_gate_up": np.stack([gate, up], 1).reshape(2 * gate.shape[0], P, F),
        "w_down": row_tiles(L0_ffn_w_down),
    }
    arrays = {name: np.ascontiguousarray(a) for name, a in arrays.items()}
    nc = bacc.Bacc("TRN2", target_bir_lowering=False, num_devices=1)
    args = [nc.dram_tensor(name, a.shape, mybir.dt.from_np(a.dtype), kind="ExternalInput").ap()
            for name, a in arrays.items()]
    out = nc.dram_tensor("out_rows", (N, F), F32, kind="ExternalOutput").ap()
    layers = [nc.dram_tensor(f"layer{g}", (N * N + P, 1), mybir.dt.int32, kind="Internal").ap() for g in range(LAYERS)]
    gnn_ffn(nc, *args, layers, out)
    result = run_bass_kernel_spmd(nc, [arrays], core_ids=[0])
    return result.results[0]["out_rows"]
```
